# Optimizing a Trainium2 kernel written in Bass

```python
import numpy as np
import jax
import jax.numpy as jnp

def _softmax(x, axis=-1):
    return jax.nn.softmax(x, axis=axis)

def _gelu(x):
    return jax.nn.gelu(x, approximate=True)

def _silu(x):
    return jax.nn.silu(x)

def _sigmoid(x):
    return jax.nn.sigmoid(x)

def _layernorm(x, axis=-1, eps=1e-05):
    m = jnp.mean(x, axis=axis, keepdims=True)
    v = jnp.var(x, axis=axis, keepdims=True)
    return (x - m) / jnp.sqrt(v + eps)

def _scatter_add(tgt, idx, src, axis=0):
    return tgt.at[idx].add(src)

def _segment_sum(src, seg, n):
    return jax.ops.segment_sum(src, seg, n)
kernel_name = 'mk_gnn_ffn_d1_gnn_r8_0e076c'

def setup_inputs(seed: int=0):
    np.random.seed(seed)
    _w = jnp.asarray

    def _rec_inputs():
        import jax
        import jax.numpy as jnp
        _gk = jax.random.key(seed)
        x = -0.0003713 + 1 * jax.random.normal(jax.random.fold_in(_gk, 1), (6250, 256), jnp.float32)
        _s = jax.random.randint(jax.random.fold_in(_gk, 2), (50000,), 0, 6250, jnp.int32)
        _d = jax.random.randint(jax.random.fold_in(_gk, 3), (50000,), 0, 6250, jnp.int32)
        _loop = jnp.arange(6250, dtype=jnp.int32)
        src = jnp.concatenate([_s, _d, _loop])
        dst = jnp.concatenate([_d, _s, _loop])
        _o = jnp.argsort(dst, stable=True)
        src = src[_o]
        dst = dst[_o]
        return (x, src, dst)
    x, src, dst = _rec_inputs()

    def _L0_gnn_setup():
        import jax, jax.numpy as jnp
        import numpy as np
        N = 6250
        E = 50000
        IN_DIM = 256
        H = 8
        D = 32
        LN_EPS = 1e-05
        key = jax.random.key(seed)
        k_x, k_e, k_w, k_a = jax.random.split(key, 4)
        x = jax.random.normal(k_x, (N, IN_DIM), dtype=jnp.float32)
        edge_index = jax.random.randint(k_e, (2, E), 0, N, dtype=jnp.int32)
        w_lim = np.sqrt(6.0 / (IN_DIM + H * D)) * np.sqrt(2.0)
        W = jax.random.uniform(k_w, (IN_DIM, H * D), minval=-w_lim, maxval=w_lim, dtype=jnp.float32)
        a_lim = np.sqrt(6.0 / (2 * D + 1))
        k_as, k_ad = jax.random.split(k_a)
        a_src = jnp.broadcast_to(jax.random.uniform(k_as, (1, D), minval=-a_lim, maxval=a_lim, dtype=jnp.float32), (H, D)).copy()
        a_dst = jnp.broadcast_to(jax.random.uniform(k_ad, (1, D), minval=-a_lim, maxval=a_lim, dtype=jnp.float32), (H, D)).copy()
        gamma = jnp.ones((H * D,), dtype=jnp.float32)
        beta = jnp.zeros((H * D,), dtype=jnp.float32)
        return {'x': x, 'edge_index': edge_index, 'W': W, 'a_src': a_src, 'a_dst': a_dst, 'gamma': gamma, 'beta': beta}
    _L0_gnn_all = _L0_gnn_setup()
    _L0_gnn_in = {k: v for k, v in _L0_gnn_all.items() if k in ('W', 'a_src', 'a_dst', 'gamma', 'beta')}
    del _L0_gnn_all

    def _L0_ffn_setup():
        import jax, jax.numpy as jnp
        import numpy as np
        TOP_K = 2
        key = jax.random.key(seed)
        ks = jax.random.split(key, 4)
        B, L, D, H, E = (8, 512, 256, 1024, 8)
        s = 0.02
        return {'x': jax.random.normal(ks[0], (B, L, D), jnp.float32), 'Wg': jax.random.normal(ks[1], (D, E), jnp.float32) * s, 'bg': jnp.zeros((E,), jnp.float32), 'W1': jax.random.normal(ks[2], (E, D, H), jnp.float32) * s, 'b1': jnp.zeros((E, H), jnp.float32), 'W2': jax.random.normal(ks[3], (E, H, D), jnp.float32) * s, 'b2': jnp.zeros((E, D), jnp.float32)}
    _L0_ffn_all = _L0_ffn_setup()
    _L0_ffn_in = {k: v for k, v in _L0_ffn_all.items() if k in ('Wg', 'bg', 'W1', 'b1', 'W2', 'b2')}
    del _L0_ffn_all
    return {'x': x, 'src': src, 'dst': dst, 'L0_gnn_W': _L0_gnn_in['W'], 'L0_gnn_a_src': _L0_gnn_in['a_src'], 'L0_gnn_a_dst': _L0_gnn_in['a_dst'], 'L0_gnn_gamma': _L0_gnn_in['gamma'], 'L0_gnn_beta': _L0_gnn_in['beta'], 'L0_ffn_Wg': _L0_ffn_in['Wg'], 'L0_ffn_bg': _L0_ffn_in['bg'], 'L0_ffn_W1': _L0_ffn_in['W1'], 'L0_ffn_b1': _L0_ffn_in['b1'], 'L0_ffn_W2': _L0_ffn_in['W2'], 'L0_ffn_b2': _L0_ffn_in['b2']}

def reference(x, src, dst, L0_gnn_W, L0_gnn_a_src, L0_gnn_a_dst, L0_gnn_gamma, L0_gnn_beta, L0_ffn_Wg, L0_ffn_bg, L0_ffn_W1, L0_ffn_b1, L0_ffn_W2, L0_ffn_b2):
    import jax
    import jax.numpy as jnp

    def _L0_gnn_ref(x, edge_index, W, a_src, a_dst, gamma, beta):
        import jax, jax.numpy as jnp
        import numpy as np
        N = 6250
        E = 50000
        IN_DIM = 256
        H = 8
        D = 32
        LN_EPS = 1e-05
        n = x.shape[0]
        src, dst = (edge_index[0], edge_index[1])
        hh = (x @ W).reshape(n, H, D)
        s_src = jnp.einsum('nhd,hd->nh', hh, a_src)
        s_dst = jnp.einsum('nhd,hd->nh', hh, a_dst)
        scores = jax.nn.leaky_relu(s_src[src] + s_dst[dst], negative_slope=0.2)
        m = jax.ops.segment_max(scores, dst, num_segments=n)
        e = jnp.exp(scores - m[dst])
        denom = jax.ops.segment_sum(e, dst, num_segments=n)
        alpha = e / denom[dst]
        msgs = hh[src] * alpha[:, :, None]
        out = jax.ops.segment_sum(msgs, dst, num_segments=n).reshape(n, H * D)
        out = out + x
        mu = jnp.mean(out, axis=-1, keepdims=True)
        var = jnp.mean(jnp.square(out - mu), axis=-1, keepdims=True)
        out = (out - mu) / jnp.sqrt(var + LN_EPS) * gamma + beta
        return jax.nn.elu(out)

    def _L0_ffn_ref(x, Wg, bg, W1, b1, W2, b2):
        import jax, jax.numpy as jnp
        import numpy as np
        TOP_K = 2
        B, L, D = x.shape
        E = W1.shape[0]
        xf = x.reshape(-1, D)
        gate_logits = xf @ Wg + bg
        top_w, top_i = jax.lax.top_k(gate_logits, TOP_K)
        top_w = jax.nn.softmax(top_w, axis=-1)
        w_dense = jnp.sum(jax.nn.one_hot(top_i, E, dtype=xf.dtype) * top_w[..., None], axis=1)
        out = jnp.zeros_like(xf)
        for e in range(E):
            h = jax.nn.gelu(xf @ W1[e] + b1[e], approximate=False)
            out = out + w_dense[:, e:e + 1] * (h @ W2[e] + b2[e])
        return out.reshape(B, L, D)
    edge_index = jnp.stack([src, dst])
    x = x + _L0_gnn_ref(_layernorm(x, axis=-1), edge_index, L0_gnn_W, L0_gnn_a_src, L0_gnn_a_dst, L0_gnn_gamma, L0_gnn_beta)
    x = x + _L0_ffn_ref(_layernorm(x, axis=-1)[None], L0_ffn_Wg, L0_ffn_bg, L0_ffn_W1, L0_ffn_b1, L0_ffn_W2, L0_ffn_b2)[0]
    return x

_drawn_inputs = setup_inputs


def setup_inputs(seed=0):
    import zlib

    import numpy as np

    out = dict(_drawn_inputs(seed))
    spreads = {'L0_gnn_gamma': (1.0, 0.2),
     'L0_gnn_beta': (0.0, 0.1),
     'L0_ffn_bg': (0.0, 0.273),
     'L0_ffn_b1': (0.0, 0.517),
     'L0_ffn_b2': (0.0, 0.1)}
    factors = {}
    for name, (base, spread) in spreads.items():
        noise = np.random.default_rng([zlib.crc32(name.encode()), seed]).standard_normal(out[name].shape)
        drawn = base * np.exp(spread * noise) if base else spread * noise
        out[name] = jnp.asarray(drawn.astype(out[name].dtype))
    for name, factor in factors.items():
        out[name] = (out[name] * factor).astype(out[name].dtype)
    return out
```

```python
from contextlib import ExitStack

import concourse.bass as bass
from concourse import mybir

F32 = mybir.dt.float32
I32 = mybir.dt.int32
U32 = mybir.dt.uint32
ALU = mybir.AluOpType
ACT = mybir.ActivationFunctionType
AX_X = mybir.AxisListType.X

P = 128
N = 6250
D = 256
H = 8
HD = D // H
NP = 125
NT = N // NP
ROW = D + H
EDGES = 106250
TB = 16
NB = -(-EDGES // (P * TB))
ET = NB * TB
NPAD = 6400
BIG = 3.0e38
EPS = 1e-5

E = 8
FF = 1024
KD, KF = D // P, FF // P
SLOT_TILES = -(-(-(-(2 * N + E * (P - 1)) // P)) // 2) * 2
NSLOT = SLOT_TILES * P
FILL = 2


class Link:

    def __init__(self, eng, sem, base=0):
        self.eng, self.sem, self.base, self.n = eng, sem, base, 0

    def __call__(self, ins):
        ins.then_inc(self.sem, 1)
        self.n += 1

    def wait(self):
        self.eng.wait_ge(self.sem, self.base + self.n)


def make_identity(nc, pool, ident, sem):
    nc.gpsimd.memset(ident[:, :], 0.0).then_inc(sem, 1)
    pool.wait_ge(sem, 1)
    nc.gpsimd.affine_select(out=ident[:, :], in_=ident[:, :], compare_op=ALU.not_equal, fill=1.0,
                            base=0, pattern=[[-1, P]], channel_multiplier=1).then_inc(sem, 1)


def node_stage(nc, x, W, a_src, a_dst, table, sdst, xnorm, slot_rows):
    with ExitStack() as ctx:
        def sb(name, shape, dt=F32):
            return ctx.enter_context(nc.sbuf_tensor(name, shape, dt))

        def sem(name):
            return ctx.enter_context(nc.semaphore(name))

        w = sb("w", [P, 2, D])
        avec = sb("avec", [P, 2, D])
        ident = sb("ident", [P, P])
        pad = sb("pad", [P, 2, H])
        blank = sb("blank", [P, FILL, D])
        xt = sb("xt", [P, 2, D])
        xn = sb("xn", [P, 2, D])
        xnT = sb("xnT", [P, 2, 2, NP])
        row = sb("row", [P, 2, ROW])
        sdr = sb("sdr", [P, 2, H])
        prod = sb("prod", [P, 2, D])
        stat = sb("stat", [P, 2, 6])
        mv = sb("mv", [P, 2, 2])
        std = sb("std", [P, 2, 1])
        rstd = sb("rstd", [P, 2, 1])
        waited = sb("waited", [P, 1])
        eps = sb("eps", [P, 1])
        psT = ctx.enter_context(nc.psum_tensor("psT", [P, 2, 512], F32))
        psH = ctx.enter_context(nc.psum_tensor("psH", [P, 2, 512], F32))

        consts = sem("consts")
        ident_made = sem("ident_made")
        pad_made = sem("pad_made")
        eps_made = sem("eps_made")
        blank_made = sem("blank_made")
        blanked = sem("blanked")
        pad_stored = sem("pad_stored")
        x_loaded = [sem("x_loaded0"), sem("x_loaded1")]
        stored = [sem("stored0"), sem("stored1")]
        dve_link = sem("dve_link")
        var_ready = sem("var_ready")
        std_ready = sem("std_ready")
        xn_ready = sem("xn_ready")
        xT_ready = sem("xT_ready")
        xT_copied = sem("xT_copied")
        hh_ready = sem("hh_ready")
        hh_copied = sem("hh_copied")
        scores_ready = sem("scores_ready")
        block = ctx.enter_context(nc.Block())

        def rows(i):
            return bass.ds(i * NP, NP)

        @block.gpsimd
        def _(pool):
            make_identity(nc, pool, ident, ident_made)
            nc.gpsimd.memset(pad[:, :, :], 0.0).then_inc(pad_made, 1)
            nc.gpsimd.memset(blank[:, :, :], 0.0).then_inc(blank_made, 1)
            nc.gpsimd.memset(eps[:, :], EPS).then_inc(eps_made, 1)

        @block.sync
        def _(sp):
            sp.dma_start(w[:, :, :], W.rearrange("(k p) n -> p k n", p=P)).then_inc(consts, 16)
            sp.dma_start(avec[:, 0, :], a_src.rearrange("h d -> (h d)")[None, :].broadcast_to([P, D])).then_inc(consts, 16)
            sp.dma_start(avec[:, 1, :], a_dst.rearrange("h d -> (h d)")[None, :].broadcast_to([P, D])).then_inc(consts, 16)
            sp.wait_ge(pad_made, 1)
            sp.dma_start(sdst[N:N + 128, :], pad[:, 0, :]).then_inc(pad_stored, 16)
            sp.dma_start(sdst[N + 128:NPAD, :], pad[0:NPAD - N - 128, 1, :]).then_inc(pad_stored, 16)
            with sp.Fori(0, NT // 2) as j:
                for b in range(2):
                    first = sp.snap((2 * j + b) * NP)
                    sp.wait_ge(xn_ready, 2 * j)
                    sp.dma_start(xt[0:NP, b, :], x[bass.ds(first, NP), :]).then_inc(x_loaded[b], 16)
            sp.wait_ge(blank_made, 1)
            for s in range(SLOT_TILES // FILL):
                sp.dma_start(slot_rows[s * FILL * P:(s + 1) * FILL * P, :].rearrange("(p f) d -> p f d", p=P),
                             blank[:, :, :]).then_inc(blanked, 16)
            sp.wait_ge(blanked, 16 * (SLOT_TILES // FILL))
            sp.wait_ge(pad_stored, 32)

        @block.scalar
        def _(act):
            act.wait_ge(eps_made, 1)

            def root(i, b):
                act.wait_ge(var_ready, i + 1)
                nc.scalar.activation(std[0:NP, b, :], mv[0:NP, b, 1:2], ACT.Sqrt, bias=eps[0:NP, :]).then_inc(std_ready, 1)

            def copies(i, b, j):
                first = act.snap(i * NP)
                act.wait_ge(stored[b], 48 * j)
                act.wait_ge(xT_ready, i + 1)
                nc.scalar.copy(xnT[:, b, :, :], psT[:, b, 0:2 * NP].rearrange("p (k n) -> p k n", k=2)).then_inc(xT_copied, 1)
                act.wait_ge(hh_ready, i + 1)
                nc.scalar.copy(row[0:NP, b, 0:D], psH[0:NP, b, 0:D]).then_inc(hh_copied, 1)
                act.wait_ge(scores_ready, i + 1)
                act.dma_start(table[bass.ds(first, NP), :], row[0:NP, b, :]).then_inc(stored[b], 16)
                act.dma_start(sdst[bass.ds(first, NP), :], sdr[0:NP, b, :]).then_inc(stored[b], 16)
                act.dma_start(xnorm[bass.ds(first, NP), :], xn[0:NP, b, :]).then_inc(stored[b], 16)

            root(0, 0)
            with act.Fori(0, NT // 2 - 1) as j:
                root(2 * j + 1, 1)
                copies(2 * j, 0, j)
                root(2 * j + 2, 0)
                copies(2 * j + 1, 1, j)
            j = NT // 2 - 1
            root(2 * j + 1, 1)
            copies(2 * j, 0, j)
            copies(2 * j + 1, 1, j)
            for b in range(2):
                act.wait_ge(stored[b], 48 * (NT // 2))

        @block.vector
        def _(dve):
            dve.wait_ge(consts, 48)

            def norm(i, b, j, before):
                link = Link(dve, dve_link, before)
                dve.wait_ge(x_loaded[b], 16 * (j + 1))
                link(nc.vector.bn_stats(stat[0:NP, b, :], xt[0:NP, b, :]))
                link.wait()
                nc.vector.memset(waited[:, :], 0.0)
                nc.vector.bn_aggr(mv[0:NP, b, :], stat[0:NP, b, :]).then_inc(var_ready, 1)
                dve.wait_ge(std_ready, i + 1)
                link(nc.vector.reciprocal(rstd[0:NP, b, :], std[0:NP, b, :]))
                link.wait()
                dve.wait_ge(stored[b], 48 * j)
                dve.wait_ge(hh_ready, 2 * j)
                nc.vector.tensor_scalar(xn[0:NP, b, :], xt[0:NP, b, :], mv[0:NP, b, 0:1], rstd[0:NP, b, :],
                                        ALU.subtract, ALU.mult).then_inc(xn_ready, 1)

            def score(i, b, j, before):
                link = Link(dve, dve_link, before)
                dve.wait_ge(hh_copied, i + 1)
                for s in range(2):
                    link(nc.vector.tensor_tensor(prod[0:NP, s, :], row[0:NP, b, 0:D], avec[0:NP, s, :], ALU.mult))
                dve.wait_ge(stored[b], 48 * j)
                link.wait()
                nc.vector.tensor_reduce(row[0:NP, b, D:ROW], prod[0:NP, 0, :].rearrange("p (h d) -> p h d", h=H), AX_X, ALU.add)
                nc.vector.tensor_reduce(sdr[0:NP, b, :], prod[0:NP, 1, :].rearrange("p (h d) -> p h d", h=H), AX_X,
                                        ALU.add).then_inc(scores_ready, 1)

            norm(0, 0, 0, 0)
            with dve.Fori(0, NT // 2 - 1) as j:
                base = 8 * j
                norm(2 * j + 1, 1, j, base + 2)
                score(2 * j, 0, j, base + 4)
                norm(2 * j + 2, 0, j + 1, base + 6)
                score(2 * j + 1, 1, j, base + 8)
            j = NT // 2 - 1
            base = 8 * j
            norm(2 * j + 1, 1, j, base + 2)
            score(2 * j, 0, j, base + 4)
            score(2 * j + 1, 1, j, base + 6)

        @block.tensor
        def _(pe):
            pe.wait_ge(consts, 48)
            pe.wait_ge(ident_made, 2)
            with pe.Fori(0, NT // 2) as j:
                for b in range(2):
                    i = 2 * j + b
                    pe.wait_ge(xn_ready, i + 1)
                    pe.wait_ge(xT_copied, 2 * j)
                    for k in range(2):
                        last = nc.tensor.transpose(psT[:, b, k * NP:(k + 1) * NP], xn[0:NP, b, k * P:(k + 1) * P], ident[0:NP, 0:NP])
                    last.then_inc(xT_ready, 1)
                    pe.wait_ge(xT_copied, i + 1)
                    pe.wait_ge(hh_copied, 2 * j)
                    for k in range(2):
                        last = nc.tensor.matmul(psH[0:NP, b, 0:D], xnT[:, b, k, :], w[:, k, :], start=(k == 0), stop=(k == 1))
                    last.then_inc(hh_ready, 1)


QT, QE = TB // 4, P // 4
FRONT_LINKS = 7
SLOTS = 4
Z_AT, C_AT, CT_AT, E_AT, G_AT = 4, 6, 8, 10, 13


def edge_stage(nc, table, sdst, srcT, dstT, dst_row, dst_prev, firsts, lasts, acc):
    with ExitStack() as ctx:
        def sb(name, shape, dt=F32):
            return ctx.enter_context(nc.sbuf_tensor(name, shape, dt))

        def psum(name):
            return ctx.enter_context(nc.psum_tensor(name, [P, 512], F32))

        def sem(name):
            return ctx.enter_context(nc.semaphore(name))

        TH = TB * H
        assert TH == P and NB % 2 == 0 and TB % SLOTS == 0
        ident = sb("ident_e", [P, P])
        iota_i = sb("iota_i", [P, 5, P], I32)
        iota_f = sb("iota_f", [P, 5, P])
        head_i = sb("head_i", [P, 1], I32)
        head = sb("head", [P, 1])
        tmask = sb("tmask", [P, TB])
        hsel = sb("hsel", [P, H])
        hselT = sb("hselT", [H, P])
        hx = sb("hx", [P, 3, P])
        first_i = sb("first_i", [P, ET], I32)
        last_i = sb("last_i", [H, ET + 1], I32)
        rel = sb("rel", [P, ET])
        node = sb("node", [P, ET])
        kc = sb("kc", [H, ET])
        idx = sb("idx", [P, 2, TB], I32)
        dbc = sb("dbc", [P, 2, TB * P], I32)
        dprev = sb("dprev", [P, 2, P + 1], I32)
        sdw = sb("sdw", [P, 2, TB, H])
        G = sb("G", [P, 2, TB, ROW])
        S = sb("S", [P, 2, TB, P])
        ST = sb("ST", [P, TB, P])
        kz = sb("kz", [P, P])
        z1 = sb("z1", [P, TH])
        z = sb("z", [P, TH])
        F = sb("F", [P, P])
        Lm = sb("Lm", [P, TB])
        Cb = sb("Cb", [H, 2, TB + 1])
        cm = sb("cm", [P, TB])
        carry = sb("carry", [P, 1])
        dz = sb("dz", [P, P + 1])
        E = sb("E", [P, P + 1])
        Xm = sb("Xm", [P, TB])
        Eb = sb("Eb", [P, 2, TH])
        Xs = sb("Xs", [P, 2, 3, TB])
        tmp = sb("tmp", [P, 3])
        waited = sb("waited_e", [P, 1])
        other = sb("other", [P, 2, P], I32)
        psA = [psum(f"psA{s}") for s in range(SLOTS)]
        psD = psum("psD")
        psZ = psum("psZ")
        psC = psum("psC")
        psE = psum("psE")

        ident_made = sem("ident_made_e")
        iota_made = sem("iota_made")
        tmask_made = sem("tmask_made")
        index_loaded = sem("index_loaded")
        idx_loaded = [sem(f"idx_loaded{b}") for b in range(2)]
        dst_loaded = [sem(f"dst_loaded{b}") for b in range(2)]
        sdw_loaded = [sem(f"sdw_loaded{b}") for b in range(2)]
        gathered = [sem(f"gathered{b}") for b in range(2)]
        dve_link = sem("dve_link_e")
        hsel_made = sem("hsel_made")
        hselT_ready = sem("hselT_ready")
        hselT_copied = sem("hselT_copied")
        marks_made = [sem(f"marks_made{b}") for b in range(2)]
        ST_made = sem("ST_made")
        sd_used = [sem(f"sd_used{b}") for b in range(2)]
        z_ready = sem("z_ready")
        zT_ready = sem("zT_ready")
        L_ready = sem("L_ready")
        C_ready = sem("C_ready")
        Cb_ready = sem("Cb_ready")
        CT_ready = sem("CT_ready")
        dz_ready = sem("dz_ready")
        E_ready = sem("E_ready")
        Xm_ready = sem("Xm_ready")
        EX_ready = sem("EX_ready")
        EX_copied = sem("EX_copied")
        G_scaled = sem("G_scaled")
        G_used = [[sem(f"G_used{b}_{c}") for c in range(4)] for b in range(2)]
        other_made = [sem(f"other_made{b}") for b in range(2)]
        acc_ready = sem("acc_ready")
        acc_copied = sem("acc_copied")
        col_done = [sem(f"col_done{s}") for s in range(SLOTS)]
        block = ctx.enter_context(nc.Block())

        def tiles(i):
            return bass.ds(i * TB, TB)

        def wait(eng, s, value):
            if not isinstance(value, int) or value > 0:
                eng.wait_ge(s, value)

        def run(eng, front, tile, begin=lambda i: None):
            steps_at = {0: 0, Z_AT: 1, C_AT: 2, CT_AT: 3, E_AT: 4, G_AT: 5}

            def both(i, b, q):
                begin(i)
                for t in range(TB):
                    if t in steps_at:
                        front(i + 1, 1 - b, q + b, steps_at[t])
                    tile(i, b, t)

            for s in range(6):
                front(0, 0, 0, s)
            with eng.Fori(0, NB // 2 - 1) as j:
                both(2 * j, 0, j)
                both(2 * j + 1, 1, j)
            both(NB - 2, 0, NB // 2 - 1)
            begin(NB - 1)
            for t in range(TB):
                tile(NB - 1, 1, t)

        @block.gpsimd
        def _(pool):
            make_identity(nc, pool, ident, ident_made)
            nc.gpsimd.iota(iota_i[:, 0, :], pattern=[[1, P]], base=0, channel_multiplier=0).then_inc(iota_made, 1)
            for k in range(2):
                nc.gpsimd.iota(iota_i[:, 1 + k, :], pattern=[[1, P // HD], [0, HD]], base=k * (P // HD),
                               channel_multiplier=0).then_inc(iota_made, 1)
            nc.gpsimd.iota(iota_i[:, 3, :], pattern=[[0, P // H], [1, H]], base=0, channel_multiplier=0).then_inc(iota_made, 1)
            nc.gpsimd.iota(iota_i[:, 4, :], pattern=[[0, P]], base=0, channel_multiplier=1).then_inc(iota_made, 1)
            nc.gpsimd.memset(tmask[:, :], 1.0).then_inc(tmask_made, 1)
            pool.wait_ge(tmask_made, 1)
            nc.gpsimd.affine_select(out=tmask[:, :], in_=tmask[:, :], compare_op=ALU.is_ge, fill=0.0, base=0,
                                    pattern=[[-H, TB]], channel_multiplier=1).then_inc(tmask_made, 1)
            pool.wait_ge(tmask_made, 2)
            nc.gpsimd.affine_select(out=tmask[:, :], in_=tmask[:, :], compare_op=ALU.is_ge, fill=0.0, base=H - 1,
                                    pattern=[[H, TB]], channel_multiplier=-1).then_inc(tmask_made, 1)
            with pool.Fori(0, NB // 2) as j:
                for b in range(2):
                    pool.wait_ge(idx_loaded[b], 16 * (j + 1))
                    pool.wait_ge(dst_loaded[b], 32 * (j + 1))
                    for t in range(TB):
                        if t % QT == 0:
                            pool.wait_ge(G_used[b][t // QT], j)
                            q = t // QT * QE
                            nc.gpsimd.tensor_tensor(other[:, b, q:q + QE], dprev[:, b, q + 1:q + QE + 1], dprev[:, b, q:q + QE],
                                                    ALU.subtract).then_inc(other_made[b], 1)
                        nc.gpsimd.indirect_dma_start(G[:, b, t, :], None, table,
                                                     bass.IndirectOffsetOnAxis(idx[:, b, t:t + 1], 0)).then_inc(gathered[b], 16)

        @block.sync
        def _(sp):
            sp.dma_start(first_i[:, :], firsts[None, :].broadcast_to([P, ET])).then_inc(index_loaded, 16)
            sp.dma_start(last_i[:, :], lasts[None, :].broadcast_to([H, ET + 1])).then_inc(index_loaded, 16)
            sp.dma_start(rel[:, :].bitcast(I32), dstT).then_inc(index_loaded, 16)
            sp.wait_ge(index_loaded, 48)
            with sp.Fori(0, NB // 2) as j:
                for b in range(2):
                    i = 2 * j + b
                    at = sp.snap(i * TB)
                    at_edge = sp.snap(i * (TB * P))
                    at_row = sp.snap(i * TH)
                    sp.wait_ge(gathered[b], 16 * TB * j)
                    sp.dma_start(idx[:, b, :], srcT[:, bass.ds(at, TB)]).then_inc(idx_loaded[b], 16)
                    sp.wait_ge(marks_made[b], j)
                    sp.dma_start(dbc[:, b, :], dst_row[None, bass.ds(at_edge, TB * P)].broadcast_to([P, TB * P])).then_inc(dst_loaded[b], 16)
                    sp.dma_start(dprev[:, b, :], dst_prev[bass.ds(at_row, TH), :]).then_inc(dst_loaded[b], 16)
                    for t in range(TB):
                        first = sp.value_load(first_i[0:1, bass.ds(at + t, 1)], min_val=0, max_val=N)
                        if t == 0:
                            sp.wait_ge(sd_used[b], j)
                        sp.dma_start(sdw[:, b, t, :], sdst[bass.ds(first, P), :]).then_inc(sdw_loaded[b], 16)

        @block.scalar
        def _(act):
            def front(i, b, q, step):
                if step == 4:
                    act.wait_ge(dz_ready, i + 1)
                    nc.scalar.activation(E[:, :], dz[:, :], ACT.Exp).then_inc(E_ready, 1)
                if step == 5:
                    act.wait_ge(EX_ready, i + 1)
                    wait(act, acc_ready, TB * (i - 1))
                    wait(act, col_done[SLOTS - 1], TB // SLOTS * (i - 1))
                    nc.scalar.copy(Eb[:, b, :], psE[:, 0:TH])
                    nc.scalar.copy(Xs[:, b, :, :], psE[:, TH:TH + 3 * TB].rearrange("p (k t) -> p k t", k=3)).then_inc(EX_copied, 1)

            def tile(i, b, t):
                first = act.value_load(first_i[0:1, bass.ds(i * TB + t, 1)], min_val=0, max_val=N)
                act.wait_ge(acc_ready, TB * i + t + 1)
                wait(act, acc_copied, TB * i + t)
                nc.scalar.copy(acc[:, :, bass.ds(first + 1, P - 1)],
                               psA[t % SLOTS][:, 0:3 * P].rearrange("p (k n) -> p k n", k=3)[:, :, 1:P]).then_inc(acc_copied, 1)

            act.wait_ge(hselT_ready, 1)
            nc.scalar.copy(hselT[:, :], psC[0:H, 0:P]).then_inc(hselT_copied, 1)
            act.wait_ge(index_loaded, 48)
            run(act, front, tile)

        @block.vector
        def _(dve):
            setup = Link(dve, dve_link)
            setup(nc.vector.memset(acc[:, :, :], 0.0))
            setup.wait()
            dve.wait_ge(iota_made, 5)
            setup(nc.vector.tensor_copy(iota_f[:, :, :], iota_i[:, :, :]))
            setup.wait()
            setup(nc.vector.tensor_single_scalar(head_i[:, :], iota_i[:, 4, 0:1], H - 1, ALU.bitwise_and))
            setup.wait()
            setup(nc.vector.tensor_copy(head[:, :], head_i[:, :]))
            setup.wait()
            setup(nc.vector.tensor_scalar(hx[:, :, :], iota_f[:, 1:4, :], head[:, :], None, ALU.is_equal))
            nc.vector.tensor_scalar(hsel[:, :], iota_f[:, 0, 0:H], head[:, :], None, ALU.is_equal).then_inc(hsel_made, 1)
            dve.wait_ge(index_loaded, 48)
            setup(nc.vector.tensor_tensor(kc[:, :], last_i[:, 1:ET + 1], last_i[:, 0:ET], ALU.not_equal))
            setup.wait()
            setup(nc.vector.tensor_scalar(kc[:, :], kc[:, :], -BIG, None, ALU.mult))
            setup(nc.vector.tensor_tensor(rel[:, :], rel[:, :].bitcast(I32), first_i[:, :], ALU.subtract))
            setup(nc.vector.tensor_scalar(node[:, :], first_i[:, :], iota_f[:, 4, 0:1], None, ALU.add))
            setup(nc.vector.memset(Cb[:, :, :], 0.0))
            for s in range(SLOTS):
                setup(nc.vector.memset(psA[s][:, 2 * P:3 * P], 0.0))
            setup.wait()
            dve.wait_ge(tmask_made, 3)
            dve.wait_ge(hselT_copied, 1)

            SETUP = setup.n
            BATCH = FRONT_LINKS + 2 * TB
            link = Link(dve, dve_link, SETUP)

            def begin(i):
                link.base, link.n = SETUP + FRONT_LINKS + i * BATCH, 0

            def front(i, b, q, step):
                if step == 0:
                    dve.wait_ge(dst_loaded[b], 32 * (q + 1))
                    wait(dve, sd_used[1 - b], q + b)
                    nc.vector.tensor_tensor(ST[:, :, :], dbc[:, b, :].rearrange("p (t e) -> p t e", t=TB),
                                            node[:, tiles(i)][:, :, None].broadcast_to([P, TB, P]), ALU.is_equal).then_inc(ST_made, 1)
                    wait(dve, acc_ready, TB * (i - 1))
                    nc.vector.tensor_tensor(S[:, b, :, :], iota_f[:, 0:1, :].broadcast_to([P, TB, P]),
                                            rel[:, tiles(i)][:, :, None].broadcast_to([P, TB, P]), ALU.is_equal)
                if step == 1:
                    dve.wait_ge(other_made[b], 4 * (q + 1))
                    nc.vector.tensor_scalar(kz[:, :], other[:, b, :], 0.0, -BIG, ALU.not_equal, ALU.mult).then_inc(marks_made[b], 1)
                    dve.wait_ge(gathered[b], 16 * TB * (q + 1))
                    dve.wait_ge(sd_used[b], q + 1)
                    link(nc.vector.tensor_tensor(z1[:, :].rearrange("p (t h) -> p t h", t=TB), G[:, b, :, D:ROW],
                                                 psD[:, 0:TH].rearrange("p (t h) -> p t h", t=TB), ALU.add))
                    link.wait()
                    wait(dve, zT_ready, i)
                    nc.vector.scalar_tensor_tensor(out=z[:, :], in0=z1[:, :], scalar=0.2, in1=z1[:, :],
                                                   op0=ALU.mult, op1=ALU.max).then_inc(z_ready, 1)
                if step == 2:
                    dve.wait_ge(zT_ready, i + 1)
                    dve.wait_ge(marks_made[b], q + 1)
                    link(nc.vector.tensor_tensor_scan(F[:, :], kz[:, :], psZ[:, 0:P], -BIG, ALU.add, ALU.max))
                    link.wait()
                    nc.vector.tensor_scalar(Lm[:, :], tmask[:, :], F[:, P - 1:P], None, ALU.mult).then_inc(L_ready, 1)
                if step == 3:
                    dve.wait_ge(C_ready, i + 1)
                    link(nc.vector.tensor_copy(Cb[:, b, 0:1], Cb[:, 1 - b, TB:TB + 1]))
                    link.wait()
                    nc.vector.tensor_tensor_scan(Cb[:, b, 1:TB + 1], kc[:, tiles(i)], psC[0:H, 0:TB], Cb[:, b, 0:1],
                                                 ALU.add, ALU.max).then_inc(Cb_ready, 1)
                if step == 4:
                    dve.wait_ge(CT_ready, i + 1)
                    link(nc.vector.tensor_tensor(cm[:, :], psC[:, P:P + TB], tmask[:, :], ALU.mult))
                    link.wait()
                    link(nc.vector.tensor_reduce(carry[:, :], cm[:, :], AX_X, ALU.add))
                    link.wait()
                    link(nc.vector.tensor_tensor_scan(F[:, :], kz[:, :], psZ[:, 0:P], carry[:, :], ALU.add, ALU.max))
                    link.wait()
                    link(nc.vector.tensor_tensor_scan(F[:, P - 2::-1], kz[:, P - 1:0:-1], F[:, P - 2::-1], F[:, P - 1:P],
                                                      ALU.add, ALU.max))
                    link.wait()
                    nc.vector.scalar_tensor_tensor(out=dz[:, P:P + 1], in0=carry[:, :], scalar=kz[:, 0:1], in1=F[:, 0:1],
                                                   op0=ALU.add, op1=ALU.subtract)
                    nc.vector.tensor_tensor(dz[:, 0:P], psZ[:, 0:P], F[:, :], ALU.subtract).then_inc(dz_ready, 1)
                    dve.wait_ge(E_ready, i + 1)
                    nc.vector.tensor_scalar(Xm[:, :], tmask[:, :], E[:, P:P + 1], None, ALU.mult).then_inc(Xm_ready, 1)
                if step == 5:
                    dve.wait_ge(EX_copied, i + 1)
                    rows = G[:, b, :, 0:D].rearrange("p t (h d) -> p t h d", h=H)
                    nc.vector.tensor_tensor(rows, rows, Eb[:, b, :].rearrange("p (t h) -> p t h", t=TB)[:, :, :, None]
                                            .broadcast_to([P, TB, H, HD]), ALU.mult).then_inc(G_scaled, 1)

            def tile(i, b, t):
                first = dve.value_load(first_i[0:1, bass.ds(i * TB + t, 1)], min_val=0, max_val=N)
                dve.wait_ge(acc_copied, TB * i + t + 1)
                link.wait()
                link(nc.vector.tensor_tensor(tmp[:, :], acc[:, :, bass.ds(first, 1)].rearrange("p k n -> p (k n)"), Xs[:, b, :, t], ALU.mult))
                link.wait()
                link(nc.vector.tensor_tensor(acc[:, :, bass.ds(first, 1)].rearrange("p k n -> p (k n)"), tmp[:, :],
                                             psA[t % SLOTS][:, 0:3 * P:P], ALU.add))
                link.wait()
                nc.vector.memset(waited[:, :], 0.0).then_inc(col_done[t % SLOTS], 1)

            run(dve, front, tile, begin)

        @block.tensor
        def _(pe):
            pe.wait_ge(ident_made, 2)
            pe.wait_ge(hsel_made, 1)
            nc.tensor.transpose(psC[0:H, 0:P], hsel[:, :], ident[:, :]).then_inc(hselT_ready, 1)
            pe.wait_ge(hselT_copied, 1)

            def front(i, b, q, step):
                if step == 0:
                    pe.wait_ge(sdw_loaded[b], 16 * TB * (q + 1))
                    pe.wait_ge(ST_made, i + 1)
                    wait(pe, z_ready, i)
                    for t in range(TB):
                        last = nc.tensor.matmul(psD[:, t * H:(t + 1) * H], ST[:, t, :], sdw[:, b, t, :], start=True, stop=True)
                    last.then_inc(sd_used[b], 1)
                if step == 1:
                    pe.wait_ge(z_ready, i + 1)
                    wait(pe, dz_ready, i)
                    nc.tensor.transpose(psZ[:, 0:P], z[:, :], ident[:, :]).then_inc(zT_ready, 1)
                if step == 2:
                    pe.wait_ge(L_ready, i + 1)
                    nc.tensor.matmul(psC[0:H, 0:TB], hsel[:, :], Lm[:, :], start=True, stop=True).then_inc(C_ready, 1)
                if step == 3:
                    pe.wait_ge(Cb_ready, i + 1)
                    nc.tensor.matmul(psC[:, P:P + TB], hselT[:, :], Cb[:, b, 0:TB], start=True, stop=True).then_inc(CT_ready, 1)
                if step == 4:
                    pe.wait_ge(Xm_ready, i + 1)
                    wait(pe, EX_copied, i)
                    nc.tensor.transpose(psE[:, 0:TH], E[:, 0:P], ident[:, :])
                    for k in range(3):
                        last = nc.tensor.matmul(psE[:, TH + k * TB:TH + (k + 1) * TB], hx[:, k, :], Xm[:, :], start=True, stop=True)
                    last.then_inc(EX_ready, 1)

            def tile(i, b, t):
                if t == 0:
                    pe.wait_ge(G_scaled, i + 1)
                wait(pe, col_done[t % SLOTS], TB // SLOTS * i + t // SLOTS)
                for k in range(3):
                    lhs = G[:, b, t, k * P:(k + 1) * P] if k < 2 else Eb[:, b, t * H:(t + 1) * H]
                    out = psA[t % SLOTS][0:P if k < 2 else H, k * P:(k + 1) * P]
                    last = nc.tensor.matmul(out, lhs, S[:, b, t, :], start=True, stop=True)
                    if k == 1 and t % QT == QT - 1:
                        last.then_inc(G_used[b][t // QT], 1)
                last.then_inc(acc_ready, 1)

            run(pe, front, tile)


def settle_stage(nc, acc, xnorm, x, gamma, beta, Wg, bg, xall, logits, x2):
    with ExitStack() as ctx:
        def sb(name, shape, dt=F32):
            return ctx.enter_context(nc.sbuf_tensor(name, shape, dt))

        def psum(name):
            return ctx.enter_context(nc.psum_tensor(name, [P, 2, 512], F32))

        def sem(name):
            return ctx.enter_context(nc.semaphore(name))

        ident = sb("ident_s", [P, P])
        gb = sb("gb", [P, 2, D])
        wg = sb("wg", [P, KD, E])
        bgb = sb("bgb", [P, E])
        mhalf = sb("mhalf", [P, 1])
        stage = sb("stage", [P, 2, 3, NP])
        xn = sb("xn_s", [P, 2, D])
        xt = sb("xt_s", [P, 2, D])
        rl = sb("rl", [P, H])
        o = sb("o", [P, D])
        o2 = sb("o2", [P, D])
        t0 = sb("t0", [P, D])
        t1 = sb("t1", [P, D])
        t2 = sb("t2", [P, D])
        u = sb("u", [P, D])
        ex = sb("ex", [P, D])
        v = sb("v", [P, D])
        x2s = sb("x2s", [P, 2, D])
        xn2 = sb("xn2", [P, 2, D])
        xT = sb("xT_s", [P, 2, KD, NP])
        stat = sb("stat_s", [P, 6])
        mv = sb("mv_s", [P, 2, 2])
        ve = sb("ve", [P, 2])
        rstd = sb("rstd_s", [P, 2])
        waited = sb("waited_s", [P, 1])
        psF = psum("psF")
        psX = psum("psX")
        psL = psum("psL")

        ident_made = sem("ident_made_s")
        consts = sem("consts_s")
        mhalf_made = sem("mhalf_made")
        in_loaded = [sem(f"in_loaded{b}") for b in range(2)]
        stage_ready = sem("stage_ready")
        f_ready = sem("f_ready")
        f_used = sem("f_used")
        link_s = sem("link_s")
        ve_ready = sem("ve_ready")
        rstd_ready = sem("rstd_ready")
        u_ready = sem("u_ready")
        ex_ready = sem("ex_ready")
        x_used = [sem(f"x_used{b}") for b in range(2)]
        x2_stored = [sem(f"x2_stored{b}") for b in range(2)]
        xn2_ready = sem("xn2_ready")
        xn2_copied = sem("xn2_copied")
        xT_ready = sem("xT_ready_s")
        xT_copied = sem("xT_copied_s")
        l_ready = sem("l_ready")
        l_used = sem("l_used")
        block = ctx.enter_context(nc.Block())

        def wait(eng, s, value):
            if not isinstance(value, int) or value > 0:
                eng.wait_ge(s, value)

        def run(eng, main, late):
            main(0, 0, 0)
            with eng.Fori(0, NT // 2 - 1) as j:
                main(2 * j + 1, 1, j)
                late(2 * j, 0, j)
                main(2 * j + 2, 0, j + 1)
                late(2 * j + 1, 1, j)
            main(NT - 1, 1, NT // 2 - 1)
            late(NT - 2, 0, NT // 2 - 1)
            late(NT - 1, 1, NT // 2 - 1)

        @block.gpsimd
        def _(pool):
            make_identity(nc, pool, ident, ident_made)
            nc.gpsimd.memset(mhalf[:, :], -0.5).then_inc(mhalf_made, 1)
            pool.wait_ge(mhalf_made, 1)
            with pool.Fori(0, NT) as i:
                for n in range(2):
                    pool.wait_ge(ve_ready, 2 * i + n + 1)
                    nc.gpsimd.tensor_tensor(rstd[0:NP, n:n + 1], ve[0:NP, n:n + 1], mhalf[0:NP, :], ALU.pow).then_inc(rstd_ready, 1)

        @block.sync
        def _(sp):
            sp.dma_start(gb[:, 0, :], gamma[None, :].broadcast_to([P, D])).then_inc(consts, 16)
            sp.dma_start(gb[:, 1, :], beta[None, :].broadcast_to([P, D])).then_inc(consts, 16)
            sp.dma_start(bgb[:, :], bg[None, :].broadcast_to([P, E])).then_inc(consts, 16)
            sp.dma_start(wg[:, :, :], Wg.rearrange("(k p) e -> p k e", p=P)).then_inc(consts, 16)
            with sp.Fori(0, NT // 2) as j:
                for b in range(2):
                    first = sp.snap((2 * j + b) * NP)
                    sp.wait_ge(x_used[b], j)
                    sp.dma_start(xn[0:NP, b, :], xnorm[bass.ds(first, NP), :]).then_inc(in_loaded[b], 16)
                    sp.dma_start(xt[0:NP, b, :], x[bass.ds(first, NP), :]).then_inc(in_loaded[b], 16)

        @block.scalar
        def _(act):
            def fetch(i, b):
                first = act.snap(i * NP) if not isinstance(i, int) else i * NP
                wait(act, f_ready, i - 1)
                nc.scalar.copy(stage[:, b, :, :], acc[:, :, bass.ds(first, NP)]).then_inc(stage_ready, 1)

            def main(i, b, q):
                if not isinstance(i, int) or i + 1 < NT:
                    fetch(i + 1, 1 - b)
                act.wait_ge(u_ready, i + 1)
                nc.scalar.activation(ex[0:NP, :], u[0:NP, :], ACT.Exp).then_inc(ex_ready, 1)

            def late(i, b, q):
                first = act.snap(i * NP) if not isinstance(i, int) else i * NP
                act.wait_ge(xn2_ready, i + 1)
                act.dma_start(x2[bass.ds(first, NP), :], x2s[0:NP, b, :]).then_inc(x2_stored[b], 16)
                nc.scalar.copy(xall[0:NP, bass.ds(i, 1), :].rearrange("p a d -> p (a d)"), xn2[0:NP, b, :]).then_inc(xn2_copied, 1)
                act.wait_ge(xT_ready, i + 1)
                nc.scalar.copy(xT[:, b, :, :], psX[:, b, 0:KD * NP].rearrange("p (k n) -> p k n", k=KD)).then_inc(xT_copied, 1)

            fetch(0, 0)
            run(act, main, late)
            for b in range(2):
                act.wait_ge(x2_stored[b], 16 * (NT // 2))

        MAIN_LINKS = 11

        @block.vector
        def _(dve):
            dve.wait_ge(consts, 64)
            link = Link(dve, link_s)

            def norm(src, out, n, i, done=None):
                link(nc.vector.bn_stats(stat[0:NP, :], src))
                link.wait()
                nc.vector.memset(waited[:, :], 0.0)
                link(nc.vector.bn_aggr(mv[0:NP, n, :], stat[0:NP, :]))
                link.wait()
                nc.vector.tensor_scalar(ve[0:NP, n:n + 1], mv[0:NP, n, 1:2], EPS, None, ALU.add).then_inc(ve_ready, 1)
                dve.wait_ge(rstd_ready, 2 * i + n + 1)
                ins = nc.vector.tensor_scalar(out, src, mv[0:NP, n, 0:1], rstd[0:NP, n:n + 1], ALU.subtract, ALU.mult)
                if done is None:
                    link(ins)
                    link.wait()
                else:
                    ins.then_inc(done, 1)

            def main(i, b, q):
                link.base, link.n = i * MAIN_LINKS, 0
                dve.wait_ge(f_ready, i + 1)
                link(nc.vector.reciprocal(rl[0:NP, :], psF[0:NP, b, 2 * P:2 * P + H]))
                link.wait()
                nc.vector.tensor_tensor(o[0:NP, :].rearrange("p (h d) -> p h d", h=H),
                                        psF[0:NP, b, 0:D].rearrange("p (h d) -> p h d", h=H),
                                        rl[0:NP, :, None].broadcast_to([NP, H, HD]), ALU.mult).then_inc(f_used, 1)
                dve.wait_ge(f_used, i + 1)
                dve.wait_ge(in_loaded[b], 32 * (q + 1))
                link(nc.vector.tensor_tensor(o2[0:NP, :], o[0:NP, :], xn[0:NP, b, :], ALU.add))
                link.wait()
                norm(o2[0:NP, :], t0[0:NP, :], 0, i)
                link(nc.vector.tensor_tensor(t1[0:NP, :], t0[0:NP, :], gb[0:NP, 0, :], ALU.mult))
                link.wait()
                link(nc.vector.tensor_tensor(t2[0:NP, :], t1[0:NP, :], gb[0:NP, 1, :], ALU.add))
                link.wait()
                nc.vector.tensor_scalar(u[0:NP, :], t2[0:NP, :], 0.0, None, ALU.min).then_inc(u_ready, 1)
                link(nc.vector.scalar_tensor_tensor(out=v[0:NP, :], in0=t2[0:NP, :], scalar=0.0, in1=xt[0:NP, b, :],
                                                    op0=ALU.max, op1=ALU.add))
                link.wait()
                nc.vector.memset(waited[:, :], 0.0).then_inc(x_used[b], 1)
                dve.wait_ge(ex_ready, i + 1)
                wait(dve, x2_stored[b], 16 * q)
                link(nc.vector.scalar_tensor_tensor(out=x2s[0:NP, b, :], in0=ex[0:NP, :], scalar=-1.0, in1=v[0:NP, :],
                                                    op0=ALU.add, op1=ALU.add))
                link.wait()
                wait(dve, xn2_copied, i - 1)
                wait(dve, xT_ready, i - 1)
                norm(x2s[0:NP, b, :], xn2[0:NP, b, :], 1, i, xn2_ready)

            def late(i, b, q):
                dve.wait_ge(l_ready, i + 1)
                nc.vector.tensor_tensor(logits[0:NP, :, bass.ds(i, 1)].rearrange("p e a -> p (e a)"), psL[0:NP, b, 0:E],
                                        bgb[0:NP, :], ALU.add).then_inc(l_used, 1)

            run(dve, main, late)

        @block.tensor
        def _(pe):
            pe.wait_ge(ident_made, 2)
            pe.wait_ge(consts, 64)

            def main(i, b, q):
                pe.wait_ge(stage_ready, i + 1)
                wait(pe, f_used, i - 1)
                for k in range(3):
                    last = nc.tensor.transpose(psF[0:NP, b, k * P:(k + 1) * P], stage[:, b, k, :], ident[:, :])
                last.then_inc(f_ready, 1)

            def late(i, b, q):
                pe.wait_ge(xn2_ready, i + 1)
                wait(pe, xT_copied, i)
                for k in range(KD):
                    last = nc.tensor.transpose(psX[:, b, k * NP:(k + 1) * NP], xn2[0:NP, b, k * P:(k + 1) * P], ident[0:NP, 0:NP])
                last.then_inc(xT_ready, 1)
                pe.wait_ge(xT_copied, i + 1)
                wait(pe, l_used, i)
                for k in range(KD):
                    last = nc.tensor.matmul(psL[0:NP, b, 0:E], xT[:, b, k, :], wg[:, k, :], start=(k == 0), stop=(k == KD - 1))
                last.then_inc(l_ready, 1)

            run(pe, main, late)


def route_stage(nc, logits, xall, slot_rows, gates, pos, tile_expert, b2, b2b):
    with ExitStack() as ctx:
        def sb(name, shape, dt=F32):
            return ctx.enter_context(nc.sbuf_tensor(name, shape, dt))

        def sem(name):
            return ctx.enter_context(nc.semaphore(name))

        ET_ = [P, E, NT]
        rank_i = sb("rank_i", [P, E], I32)
        rank_f = sb("rank_f", [P, E])
        slot_i = sb("slot_i", [P, SLOT_TILES], I32)
        slot_f = sb("slot_f", [P, SLOT_TILES])
        tri = sb("tri", [P, P])
        ones = sb("ones", [P, P])
        top = sb("top", [P, 2, NT])
        hit = sb("hit", ET_)
        code = sb("code", ET_)
        best = sb("best", [P, NT])
        mark = sb("mark", [P, 2, E, NT])
        rest = sb("rest", ET_)
        both = sb("both", ET_)
        total = sb("total", ET_)
        keep = sb("keep", ET_)
        run_ = sb("run", ET_)
        place = sb("place", ET_)
        size_i = sb("size_i", [P, E], I32)
        size_j = sb("size_j", [P, E], I32)
        size = sb("size", [P, E])
        end = sb("end", [P, E])
        start = sb("start", [P, E])
        zero = sb("zero", [P, E])
        diff = sb("diff", [P, NT])
        e2 = sb("e2", [P, NT])
        den = sb("den", [P, NT])
        posf = sb("posf", [P, 2, NT])
        over = sb("over", [P, SLOT_TILES, E])
        count = sb("count", [P, SLOT_TILES])
        psR = ctx.enter_context(nc.psum_tensor("psR", [P, 512], F32))
        psT = ctx.enter_context(nc.psum_tensor("psTot", [P, 512], F32))

        made = sem("made")
        shifted = sem("shifted")
        tri_made = sem("tri_made")
        step = sem("step")
        diff_ready = sem("diff_ready")
        e2_ready = sem("e2_ready")
        both_ready = sem("both_ready")
        ranks_ready = sem("ranks_ready")
        pos_ready = sem("pos_ready")
        scattered = sem("scattered")
        loaded = sem("biases_loaded")
        block = ctx.enter_context(nc.Block())
        A = slice(0, NP)

        @block.sync
        def _(sp):
            sp.dma_start(b2b[:, :], b2.rearrange("e d -> (e d)")[None, :].broadcast_to([P, E * D])).then_inc(loaded, 16)
            sp.wait_ge(loaded, 16)

        @block.gpsimd
        def _(pool):
            nc.gpsimd.iota(rank_i[:, :], pattern=[[-1, E]], base=E, channel_multiplier=0).then_inc(made, 1)
            nc.gpsimd.iota(slot_i[:, :], pattern=[[P, SLOT_TILES]], base=0, channel_multiplier=0).then_inc(made, 1)
            nc.gpsimd.memset(ones[:, :], 1.0).then_inc(made, 1)
            nc.gpsimd.memset(tri[:, :], 1.0).then_inc(tri_made, 1)
            pool.wait_ge(tri_made, 1)
            nc.gpsimd.affine_select(out=tri[:, :], in_=tri[:, :], compare_op=ALU.is_gt, fill=0.0, base=0,
                                    pattern=[[1, P]], channel_multiplier=-1).then_inc(tri_made, 1)
            pool.wait_ge(pos_ready, 1)
            for t in range(NT):
                for k in range(2):
                    nc.gpsimd.indirect_dma_start(slot_rows, bass.IndirectOffsetOnAxis(pos[A, k, t:t + 1], 0), xall[A, t, :],
                                                 None).then_inc(scattered, 16)
            pool.wait_ge(scattered, 16 * 2 * NT)

        @block.scalar
        def _(act):
            act.wait_ge(diff_ready, 1)
            nc.scalar.activation(e2[A, :], diff[A, :], ACT.Exp).then_inc(e2_ready, 1)

        @block.tensor
        def _(pe):
            pe.wait_ge(tri_made, 2)
            pe.wait_ge(both_ready, 1)
            nc.tensor.matmul(psR[0:NP, 0:E * NT], tri[A, 0:NP], both[A, :, :].rearrange("p e t -> p (e t)"), start=True, stop=True)
            nc.tensor.matmul(psT[0:NP, 0:E * NT], ones[A, 0:NP], both[A, :, :].rearrange("p e t -> p (e t)"), start=True,
                             stop=True).then_inc(ranks_ready, 1)

        @block.vector
        def _(dve):
            link = Link(dve, step)

            def do(ins):
                link(ins)
                link.wait()

            V = nc.vector

            def by_t(a):
                return a.rearrange("p e t -> p t e")

            def over_e(a):
                return a[:, None, :].broadcast_to([NP, E, NT])

            dve.wait_ge(made, 3)
            do(V.tensor_copy(rank_f[:, :], rank_i[:, :]))
            do(V.tensor_copy(slot_f[:, :], slot_i[:, :]))
            src = logits
            for k in range(2):
                do(V.tensor_reduce(top[A, k, :], by_t(src[A, :, :]), AX_X, ALU.max))
                do(V.tensor_tensor(hit[A, :, :], src[A, :, :], over_e(top[A, k, :]), ALU.is_equal))
                do(V.tensor_tensor(code[A, :, :], hit[A, :, :], rank_f[A, :, None].broadcast_to([NP, E, NT]), ALU.mult))
                do(V.tensor_reduce(best[A, :], by_t(code[A, :, :]), AX_X, ALU.max))
                do(V.tensor_tensor(mark[A, k, :, :], over_e(best[A, :]), rank_f[A, :, None].broadcast_to([NP, E, NT]), ALU.is_equal))
                if k == 0:
                    do(V.scalar_tensor_tensor(out=rest[A, :, :], in0=mark[A, k, :, :], scalar=-BIG, in1=src[A, :, :],
                                              op0=ALU.mult, op1=ALU.add))
                    src = rest
            V.tensor_tensor(both[A, :, :], mark[A, 0, :, :], mark[A, 1, :, :], ALU.add).then_inc(both_ready, 1)
            V.tensor_tensor(diff[A, :], top[A, 1, :], top[A, 0, :], ALU.subtract).then_inc(diff_ready, 1)
            dve.wait_ge(e2_ready, 1)
            do(V.tensor_scalar(den[A, :], e2[A, :], 1.0, None, ALU.add))
            do(V.reciprocal(gates[A, 0, :], den[A, :]))
            do(V.tensor_tensor(gates[A, 1, :], e2[A, :], gates[A, 0, :], ALU.mult))
            dve.wait_ge(ranks_ready, 1)
            do(V.memset(keep[:, :, :], 1.0))
            do(V.memset(keep[:, :, 0:1], 0.0))
            do(V.memset(zero[:, :], 0.0))
            do(V.tensor_copy(total[A, :, :].rearrange("p e t -> p (e t)"), psT[A, 0:E * NT]))
            do(V.tensor_tensor_scan(run_[A, :, :].rearrange("p e t -> p (e t)"), keep[A, :, :].rearrange("p e t -> p (e t)"),
                                    total[A, :, :].rearrange("p e t -> p (e t)"), 0.0, ALU.mult, ALU.add))
            do(V.tensor_scalar(size_i[A, :], run_[A, :, NT - 1], float(P - 1), None, ALU.add))
            do(V.tensor_single_scalar(size_j[A, :], size_i[A, :], -P, ALU.bitwise_and))
            do(V.tensor_copy(size[A, :], size_j[A, :]))
            do(V.tensor_tensor_scan(end[A, :], size[A, :], zero[A, :], 0.0, ALU.add, ALU.add))
            do(V.tensor_tensor(start[A, :], end[A, :], size[A, :], ALU.subtract))
            do(V.tensor_tensor(place[A, :, :], run_[A, :, :], total[A, :, :], ALU.subtract))
            do(V.tensor_tensor(code[A, :, :].rearrange("p e t -> p (e t)"), place[A, :, :].rearrange("p e t -> p (e t)"),
                               psR[A, 0:E * NT], ALU.add))
            do(V.tensor_tensor(place[A, :, :], code[A, :, :], start[A, :, None].broadcast_to([NP, E, NT]), ALU.add))
            for k in range(2):
                do(V.tensor_tensor(code[A, :, :], place[A, :, :], mark[A, k, :, :], ALU.mult))
                do(V.tensor_reduce(posf[A, k, :], by_t(code[A, :, :]), AX_X, ALU.add))
            V.tensor_copy(pos[A, :, :], posf[A, :, :]).then_inc(pos_ready, 1)
            do(V.tensor_tensor(over[A, :, :], slot_f[A, :, None].broadcast_to([NP, SLOT_TILES, E]),
                               end[A, None, :].broadcast_to([NP, SLOT_TILES, E]), ALU.is_ge))
            do(V.tensor_reduce(count[A, :], over[A, :, :], AX_X, ALU.add))
            do(V.tensor_scalar(tile_expert[A, :], count[A, :], float(E - 1), None, ALU.min))


def expert_stage(nc, slot_rows, slot_out, tile_expert, W1, b1, W2, b2b):
    with ExitStack() as ctx:
        def sb(name, shape, dt=F32):
            return ctx.enter_context(nc.sbuf_tensor(name, shape, dt))

        def sem(name):
            return ctx.enter_context(nc.semaphore(name))

        ident = sb("ident_x", [P, P])
        w1 = sb("w1", [P, KD, E * FF])
        w2 = sb("w2", [P, KF, E * D])
        b1_rows = sb("b1_rows", [E * KF, P])
        b1T = sb("b1T", [P, E * KF])
        xs = sb("xs", [P, 2, D])
        xT = sb("xT_x", [P, 2, KD, P])
        hs = sb("hs", [P, FF])
        hT = sb("hT", [P, 2, KF, P])
        ys = sb("ys", [P, 2, D])
        psX = ctx.enter_context(nc.psum_tensor("psX_x", [P, 512], F32))
        psH = ctx.enter_context(nc.psum_tensor("psH_x", [P, FF // 512, 512], F32))
        psG = ctx.enter_context(nc.psum_tensor("psG", [P, FF // 512, 512], F32))
        psY = ctx.enter_context(nc.psum_tensor("psY", [P, 2, 512], F32))

        ident_made = sem("ident_made_x")
        weights = sem("weights")
        b1_loaded = sem("b1_loaded")
        b1_turned = sem("b1_turned")
        b1_copied = sem("b1_copied")
        x_loaded = [sem(f"xs_loaded{b}") for b in range(2)]
        x_used = [sem(f"xs_used{b}") for b in range(2)]
        xT_copied = sem("xT_copied_x")
        h_ready = sem("h_ready")
        h_copied = sem("h_copied")
        hT_ready = sem("hT_ready")
        gelu_done = sem("gelu_done")
        y_ready = sem("y_ready")
        y_done = sem("y_done")
        y_stored = [sem(f"y_stored{b}") for b in range(2)]
        block = ctx.enter_context(nc.Block())
        HALF = FF // 2
        MH = KF // 2

        def wait(eng, s, value):
            if not isinstance(value, int) or value > 0:
                eng.wait_ge(s, value)

        def run(eng, body):
            body(0, 0, 0, True, False)
            with eng.Fori(0, SLOT_TILES // 2 - 1) as j:
                body(2 * j + 1, 1, j, False, False)
                body(2 * j + 2, 0, j + 1, False, False)
            body(SLOT_TILES - 1, 1, SLOT_TILES // 2 - 1, False, True)

        def expert_of(eng, i):
            return eng.value_load(tile_expert[0:1, bass.ds(i, 1)], min_val=0, max_val=E - 1)

        @block.gpsimd
        def _(pool):
            make_identity(nc, pool, ident, ident_made)

        @block.sync
        def _(sp):
            sp.dma_start(b1_rows[:, :], b1.rearrange("e (m p) -> (e m) p", p=P)).then_inc(b1_loaded, 16)
            for k in range(KD):
                sp.dma_start(w1[:, k, :].rearrange("p (e n) -> p e n", e=E),
                             W1[:, k * P:(k + 1) * P, :].rearrange("e p n -> p e n")).then_inc(weights, 16)
            for m in range(KF):
                sp.dma_start(w2[:, m, :].rearrange("p (e n) -> p e n", e=E),
                             W2[:, m * P:(m + 1) * P, :].rearrange("e p n -> p e n")).then_inc(weights, 16)
            with sp.Fori(0, SLOT_TILES // 2) as j:
                for b in range(2):
                    first = sp.snap((2 * j + b) * P)
                    sp.wait_ge(x_used[b], j)
                    sp.dma_start(xs[:, b, :], slot_rows[bass.ds(first, P), :]).then_inc(x_loaded[b], 16)

        @block.scalar
        def _(act):
            def copy_x(i, b, q):
                act.wait_ge(x_used[b], q + 1)
                wait(act, h_ready, 2 * (i - 1))
                nc.scalar.copy(xT[:, b, :, :], psX[:, 0:KD * P].rearrange("p (k n) -> p k n", k=KD)).then_inc(xT_copied, 1)

            def body(i, b, q, first, last):
                if not last:
                    copy_x(i + 1, 1 - b, q + b)
                e = expert_of(act, i)
                wait(act, y_ready, i - 1)
                for n in range(2):
                    act.wait_ge(hT_ready, 2 * i + n + 1)
                    for m in range(n * MH, (n + 1) * MH):
                        done = nc.scalar.activation(hT[:, b, m, :], psG[:, n, (m - n * MH) * P:(m - n * MH + 1) * P], ACT.Gelu,
                                                    bias=b1T[:, bass.ds(e * KF + m, 1)])
                    done.then_inc(gelu_done, 1)
                if not first:
                    store(i - 1, 1 - b)

            def store(i, b):
                first_slot = i * P if isinstance(i, int) else act.snap(i * P)
                act.wait_ge(y_done, i + 1)
                act.dma_start(slot_out[bass.ds(first_slot, P), :], ys[:, b, :]).then_inc(y_stored[b], 16)

            act.wait_ge(b1_turned, 1)
            nc.scalar.copy(b1T[:, :], psY[:, 0, 0:E * KF]).then_inc(b1_copied, 1)
            act.wait_ge(b1_copied, 1)
            copy_x(0, 0, 0)
            run(act, body)
            store(SLOT_TILES - 1, 1)
            for b in range(2):
                act.wait_ge(y_stored[b], 16 * (SLOT_TILES // 2))

        @block.vector
        def _(dve):
            def finish(i, b, q):
                e = expert_of(dve, i)
                dve.wait_ge(y_ready, i + 1)
                wait(dve, y_stored[b], 16 * q)
                nc.vector.tensor_tensor(ys[:, b, :], psY[:, b, 0:D], b2b[:, bass.ds(e * D, D)], ALU.add).then_inc(y_done, 1)

            def body(i, b, q, first, last):
                for n in range(2):
                    dve.wait_ge(h_ready, 2 * i + n + 1)
                    wait(dve, hT_ready, 2 * i + n - 1 if not first else 0)
                    nc.vector.tensor_copy(hs[:, n * HALF:(n + 1) * HALF], psH[:, n, :]).then_inc(h_copied, 1)
                if not first:
                    finish(i - 1, 1 - b, q - 1 + b)

            run(dve, body)
            finish(SLOT_TILES - 1, 1, SLOT_TILES // 2 - 1)

        @block.tensor
        def _(pe):
            pe.wait_ge(ident_made, 2)

            def turn_x(i, b, q):
                pe.wait_ge(x_loaded[b], 16 * (q + 1))
                wait(pe, xT_copied, i)
                for k in range(KD):
                    done = nc.tensor.transpose(psX[:, k * P:(k + 1) * P], xs[:, b, k * P:(k + 1) * P], ident[:, :])
                done.then_inc(x_used[b], 1)

            def down(i, b, q):
                e = expert_of(pe, i)
                wait(pe, y_done, i)
                for m in range(KF):
                    if m % MH == 0:
                        pe.wait_ge(gelu_done, 2 * i + m // MH + 1)
                    done = nc.tensor.matmul(psY[:, b, 0:D], hT[:, b, m, :], w2[:, m, bass.ds(e * D, D)],
                                            start=(m == 0), stop=(m == KF - 1))
                done.then_inc(y_ready, 1)

            def body(i, b, q, first, last):
                e = expert_of(pe, i)
                pe.wait_ge(xT_copied, i + 1)
                for n in range(2):
                    wait(pe, h_copied, 2 * i + n - 1 if not first else 0)
                    for k in range(KD):
                        done = nc.tensor.matmul(psH[:, n, :], xT[:, b, k, :], w1[:, k, bass.ds(e * FF + n * HALF, HALF)],
                                                start=(k == 0), stop=(k == KD - 1))
                    done.then_inc(h_ready, 1)
                if not last:
                    turn_x(i + 1, 1 - b, q + b)
                if not first:
                    down(i - 1, 1 - b, q - 1 + b)
                for n in range(2):
                    pe.wait_ge(h_copied, 2 * i + n + 1)
                    wait(pe, gelu_done, 2 * i + n - 1 if not first else 0)
                    for m in range(n * MH, (n + 1) * MH):
                        done = nc.tensor.transpose(psG[:, n, (m - n * MH) * P:(m - n * MH + 1) * P], hs[:, m * P:(m + 1) * P],
                                                   ident[:, :])
                    done.then_inc(hT_ready, 1)

            pe.wait_ge(b1_loaded, 16)
            nc.tensor.transpose(psY[:, 0, 0:E * KF], b1_rows[:, :], ident[0:E * KF, 0:E * KF]).then_inc(b1_turned, 1)
            turn_x(0, 0, 0)
            pe.wait_ge(b1_copied, 1)
            pe.wait_ge(weights, 16 * (KD + KF))
            run(pe, body)
            down(SLOT_TILES - 1, 1, SLOT_TILES // 2 - 1)


def combine_stage(nc, slot_out, x2, gates, pos, out):
    RING = 4
    with ExitStack() as ctx:
        def sb(name, shape, dt=F32):
            return ctx.enter_context(nc.sbuf_tensor(name, shape, dt))

        def sem(name):
            return ctx.enter_context(nc.semaphore(name))

        y = sb("y_c", [P, RING, 2, D])
        xt = sb("xt_c", [P, RING, D])
        part = sb("part", [P, RING, D])
        res = sb("res", [P, RING, D])
        x_loaded = [sem(f"xc_loaded{r}") for r in range(RING)]
        y_loaded = [[sem(f"y{k}_loaded{r}") for r in range(RING)] for k in range(2)]
        half = sem("half")
        done = sem("done_c")
        stored = [sem(f"stored_c{r}") for r in range(RING)]
        block = ctx.enter_context(nc.Block())

        @block.gpsimd
        def _(pool):
            for t in range(NT):
                if t >= RING:
                    pool.wait_ge(done, t - RING + 1)
                for k in range(2):
                    nc.gpsimd.indirect_dma_start(y[0:NP, t % RING, k, :], None, slot_out,
                                                 bass.IndirectOffsetOnAxis(pos[0:NP, k, t:t + 1], 0)).then_inc(y_loaded[k][t % RING], 16)

        @block.sync
        def _(sp):
            for t in range(NT):
                if t >= RING:
                    sp.wait_ge(done, t - RING + 1)
                sp.dma_start(xt[0:NP, t % RING, :], x2[t * NP:(t + 1) * NP, :]).then_inc(x_loaded[t % RING], 16)

        @block.scalar
        def _(act):
            for t in range(NT):
                act.wait_ge(done, t + 1)
                act.dma_start(out[t * NP:(t + 1) * NP, :], res[0:NP, t % RING, :]).then_inc(stored[t % RING], 16)
            for r in range(RING):
                act.wait_ge(stored[r], 16 * len(range(r, NT, RING)))

        @block.vector
        def _(dve):
            for t in range(NT):
                r, n = t % RING, 16 * (t // RING + 1)
                dve.wait_ge(x_loaded[r], n)
                dve.wait_ge(y_loaded[0][r], n)
                nc.vector.scalar_tensor_tensor(out=part[0:NP, r, :], in0=y[0:NP, r, 0, :], scalar=gates[0:NP, 0, t:t + 1],
                                               in1=xt[0:NP, r, :], op0=ALU.mult, op1=ALU.add).then_inc(half, 1)
                dve.wait_ge(y_loaded[1][r], n)
                dve.wait_ge(half, t + 1)
                if t >= RING:
                    dve.wait_ge(stored[r], n - 16)
                nc.vector.scalar_tensor_tensor(out=res[0:NP, r, :], in0=y[0:NP, r, 1, :], scalar=gates[0:NP, 1, t:t + 1],
                                               in1=part[0:NP, r, :], op0=ALU.mult, op1=ALU.add).then_inc(done, 1)


def build(nc, x, srcT, dstT, dst_row, dst_prev, firsts, lasts, W, a_src, a_dst, gamma, beta, Wg, bg, W1, b1, W2, b2, out):
    def dram(name, shape):
        return nc.dram_tensor(name, shape, F32, kind="Internal").ap()

    table = dram("table", (N, ROW))
    sdst = dram("sdst", (NPAD, H))
    xnorm = dram("xnorm", (N, D))
    x2 = dram("x2", (N, D))
    slot_rows = dram("slot_rows", (NSLOT, D))
    slot_out = dram("slot_out", (NSLOT, D))

    node_stage(nc, x, W, a_src, a_dst, table, sdst, xnorm, slot_rows)
    with ExitStack() as routing:
        def sb(name, shape, dt=F32):
            return routing.enter_context(nc.sbuf_tensor(name, shape, dt))

        gates = sb("gates", [P, 2, NT])
        pos = sb("pos", [P, 2, NT], I32)
        tile_expert = sb("tile_expert", [P, SLOT_TILES], I32)
        b2b = sb("b2b", [P, E * D])
        with ExitStack() as graph:
            acc = graph.enter_context(nc.sbuf_tensor("acc", [P, 3, NPAD], F32))
            edge_stage(nc, table, sdst, srcT, dstT, dst_row, dst_prev, firsts, lasts, acc)
            xall = graph.enter_context(nc.sbuf_tensor("xall", [P, NT, D], F32))
            logits = graph.enter_context(nc.sbuf_tensor("logits", [P, E, NT], F32))
            settle_stage(nc, acc, xnorm, x, gamma, beta, Wg, bg, xall, logits, x2)
            route_stage(nc, logits, xall, slot_rows, gates, pos, tile_expert, b2, b2b)
        expert_stage(nc, slot_rows, slot_out, tile_expert, W1, b1, W2, b2b)
        combine_stage(nc, slot_out, x2, gates, pos, out)


def kernel(**inputs):
    import numpy as np
    import concourse.bacc as bacc
    from concourse.bass_utils import run_bass_kernel_spmd

    fill = ET * P - EDGES
    src = np.concatenate([np.asarray(inputs["src"]), np.zeros(fill, np.int32)])
    dst = np.concatenate([np.asarray(inputs["dst"]), np.full(fill, N, np.int32)])
    by_tile = dst.reshape(ET, P)
    lasts = np.concatenate([np.full(1, -1, np.int32), by_tile[:, P - 1]])
    prev = np.concatenate([lasts[:ET, None], by_tile], axis=1)
    arrays = {
        "in_x": inputs["x"],
        "in_srcT": src.reshape(ET, P).T,
        "in_dstT": by_tile.T,
        "in_dst_row": dst,
        "in_dst_prev": np.repeat(prev, H, axis=0),
        "in_firsts": by_tile[:, 0],
        "in_lasts": lasts,
    }
    for name in ("gnn_W", "gnn_a_src", "gnn_a_dst", "gnn_gamma", "gnn_beta", "ffn_Wg", "ffn_bg", "ffn_W1", "ffn_b1", "ffn_W2", "ffn_b2"):
        arrays["in_" + name] = inputs["L0_" + name]
    arrays = {k: np.ascontiguousarray(v) for k, v in arrays.items()}

    nc = bacc.Bacc("TRN2", target_bir_lowering=False, num_devices=1)
    args = [nc.dram_tensor(k, a.shape, mybir.dt.from_np(a.dtype), kind="ExternalInput").ap() for k, a in arrays.items()]
    out = nc.dram_tensor("out", (N, D), F32, kind="ExternalOutput").ap()
    build(nc, *args, out)
    r = run_bass_kernel_spmd(nc, [arrays], core_ids=[0])
    return r.results[0]["out"]
```

```python
from contextlib import ExitStack

import concourse.bass as bass
from concourse import mybir

F32 = mybir.dt.float32
I32 = mybir.dt.int32
U32 = mybir.dt.uint32
ALU = mybir.AluOpType
ACT = mybir.ActivationFunctionType
AX_X = mybir.AxisListType.X

P = 128
N = 6250
D = 256
H = 8
HD = D // H
NP = 125
NT = N // NP
ROW = D + H
EDGES = 106250
TB = 16
NB = -(-EDGES // (P * TB))
ET = NB * TB
NPAD = 6400
BIG = 3.0e38
EPS = 1e-5

E = 8
FF = 1024
KD, KF = D // P, FF // P
SLOT_TILES = -(-(-(-(2 * N + E * (P - 1)) // P)) // 2) * 2
NSLOT = SLOT_TILES * P
FILL = 2


class Link:

    def __init__(self, eng, sem, base=0):
        self.eng, self.sem, self.base, self.n = eng, sem, base, 0

    def __call__(self, ins):
        ins.then_inc(self.sem, 1)
        self.n += 1

    def wait(self):
        self.eng.wait_ge(self.sem, self.base + self.n)


def make_identity(nc, pool, ident, sem):
    nc.gpsimd.memset(ident[:, :], 0.0).then_inc(sem, 1)
    pool.wait_ge(sem, 1)
    nc.gpsimd.affine_select(out=ident[:, :], in_=ident[:, :], compare_op=ALU.not_equal, fill=1.0,
                            base=0, pattern=[[-1, P]], channel_multiplier=1).then_inc(sem, 1)


def node_stage(nc, x, W, a_src, a_dst, table, sdst, xnorm, slot_rows):
    with ExitStack() as ctx:
        def sb(name, shape, dt=F32):
            return ctx.enter_context(nc.sbuf_tensor(name, shape, dt))

        def sem(name):
            return ctx.enter_context(nc.semaphore(name))

        w = sb("w", [P, 2, D])
        avec = sb("avec", [P, 2, D])
        ident = sb("ident", [P, P])
        pad = sb("pad", [P, 2, H])
        blank = sb("blank", [P, FILL, D])
        xt = sb("xt", [P, 2, D])
        xn = sb("xn", [P, 2, D])
        xnT = sb("xnT", [P, 2, 2, NP])
        row = sb("row", [P, 2, ROW])
        sdr = sb("sdr", [P, 2, H])
        prod = sb("prod", [P, 2, D])
        stat = sb("stat", [P, 2, 6])
        mv = sb("mv", [P, 2, 2])
        std = sb("std", [P, 2, 1])
        rstd = sb("rstd", [P, 2, 1])
        waited = sb("waited", [P, 1])
        eps = sb("eps", [P, 1])
        psT = ctx.enter_context(nc.psum_tensor("psT", [P, 2, 512], F32))
        psH = ctx.enter_context(nc.psum_tensor("psH", [P, 2, 512], F32))

        consts = sem("consts")
        ident_made = sem("ident_made")
        pad_made = sem("pad_made")
        eps_made = sem("eps_made")
        blank_made = sem("blank_made")
        blanked = sem("blanked")
        pad_stored = sem("pad_stored")
        x_loaded = [sem("x_loaded0"), sem("x_loaded1")]
        stored = [sem("stored0"), sem("stored1")]
        dve_link = sem("dve_link")
        var_ready = sem("var_ready")
        std_ready = sem("std_ready")
        xn_ready = sem("xn_ready")
        xT_ready = sem("xT_ready")
        xT_copied = sem("xT_copied")
        hh_ready = sem("hh_ready")
        hh_copied = sem("hh_copied")
        scores_ready = sem("scores_ready")
        block = ctx.enter_context(nc.Block())

        def rows(i):
            return bass.ds(i * NP, NP)

        @block.gpsimd
        def _(pool):
            make_identity(nc, pool, ident, ident_made)
            nc.gpsimd.memset(pad[:, :, :], 0.0).then_inc(pad_made, 1)
            nc.gpsimd.memset(blank[:, :, :], 0.0).then_inc(blank_made, 1)
            nc.gpsimd.memset(eps[:, :], EPS).then_inc(eps_made, 1)

        @block.sync
        def _(sp):
            sp.dma_start(w[:, :, :], W.rearrange("(k p) n -> p k n", p=P)).then_inc(consts, 16)
            sp.dma_start(avec[:, 0, :], a_src.rearrange("h d -> (h d)")[None, :].broadcast_to([P, D])).then_inc(consts, 16)
            sp.dma_start(avec[:, 1, :], a_dst.rearrange("h d -> (h d)")[None, :].broadcast_to([P, D])).then_inc(consts, 16)
            sp.wait_ge(pad_made, 1)
            sp.dma_start(sdst[N:N + 128, :], pad[:, 0, :]).then_inc(pad_stored, 16)
            sp.dma_start(sdst[N + 128:NPAD, :], pad[0:NPAD - N - 128, 1, :]).then_inc(pad_stored, 16)
            with sp.Fori(0, NT // 2) as j:
                for b in range(2):
                    first = sp.snap((2 * j + b) * NP)
                    sp.wait_ge(xn_ready, 2 * j)
                    sp.dma_start(xt[0:NP, b, :], x[bass.ds(first, NP), :]).then_inc(x_loaded[b], 16)
            sp.wait_ge(blank_made, 1)
            for s in range(SLOT_TILES // FILL):
                sp.dma_start(slot_rows[s * FILL * P:(s + 1) * FILL * P, :].rearrange("(p f) d -> p f d", p=P),
                             blank[:, :, :]).then_inc(blanked, 16)
            sp.wait_ge(blanked, 16 * (SLOT_TILES // FILL))
            sp.wait_ge(pad_stored, 32)

        @block.scalar
        def _(act):
            act.wait_ge(eps_made, 1)

            def root(i, b):
                act.wait_ge(var_ready, i + 1)
                nc.scalar.activation(std[0:NP, b, :], mv[0:NP, b, 1:2], ACT.Sqrt, bias=eps[0:NP, :]).then_inc(std_ready, 1)

            def copies(i, b, j):
                first = act.snap(i * NP)
                act.wait_ge(stored[b], 48 * j)
                act.wait_ge(xT_ready, i + 1)
                nc.scalar.copy(xnT[:, b, :, :], psT[:, b, 0:2 * NP].rearrange("p (k n) -> p k n", k=2)).then_inc(xT_copied, 1)
                act.wait_ge(hh_ready, i + 1)
                nc.scalar.copy(row[0:NP, b, 0:D], psH[0:NP, b, 0:D]).then_inc(hh_copied, 1)
                act.wait_ge(scores_ready, i + 1)
                act.dma_start(table[bass.ds(first, NP), :], row[0:NP, b, :]).then_inc(stored[b], 16)
                act.dma_start(sdst[bass.ds(first, NP), :], sdr[0:NP, b, :]).then_inc(stored[b], 16)
                act.dma_start(xnorm[bass.ds(first, NP), :], xn[0:NP, b, :]).then_inc(stored[b], 16)

            root(0, 0)
            with act.Fori(0, NT // 2 - 1) as j:
                root(2 * j + 1, 1)
                copies(2 * j, 0, j)
                root(2 * j + 2, 0)
                copies(2 * j + 1, 1, j)
            j = NT // 2 - 1
            root(2 * j + 1, 1)
            copies(2 * j, 0, j)
            copies(2 * j + 1, 1, j)
            for b in range(2):
                act.wait_ge(stored[b], 48 * (NT // 2))

        @block.vector
        def _(dve):
            dve.wait_ge(consts, 48)

            def norm(i, b, j, before):
                link = Link(dve, dve_link, before)
                dve.wait_ge(x_loaded[b], 16 * (j + 1))
                link(nc.vector.bn_stats(stat[0:NP, b, :], xt[0:NP, b, :]))
                link.wait()
                nc.vector.memset(waited[:, :], 0.0)
                nc.vector.bn_aggr(mv[0:NP, b, :], stat[0:NP, b, :]).then_inc(var_ready, 1)
                dve.wait_ge(std_ready, i + 1)
                link(nc.vector.reciprocal(rstd[0:NP, b, :], std[0:NP, b, :]))
                link.wait()
                dve.wait_ge(stored[b], 48 * j)
                dve.wait_ge(hh_ready, 2 * j)
                nc.vector.tensor_scalar(xn[0:NP, b, :], xt[0:NP, b, :], mv[0:NP, b, 0:1], rstd[0:NP, b, :],
                                        ALU.subtract, ALU.mult).then_inc(xn_ready, 1)

            def score(i, b, j, before):
                link = Link(dve, dve_link, before)
                dve.wait_ge(hh_copied, i + 1)
                for s in range(2):
                    link(nc.vector.tensor_tensor(prod[0:NP, s, :], row[0:NP, b, 0:D], avec[0:NP, s, :], ALU.mult))
                dve.wait_ge(stored[b], 48 * j)
                link.wait()
                nc.vector.tensor_reduce(row[0:NP, b, D:ROW], prod[0:NP, 0, :].rearrange("p (h d) -> p h d", h=H), AX_X, ALU.add)
                nc.vector.tensor_reduce(sdr[0:NP, b, :], prod[0:NP, 1, :].rearrange("p (h d) -> p h d", h=H), AX_X,
                                        ALU.add).then_inc(scores_ready, 1)

            norm(0, 0, 0, 0)
            with dve.Fori(0, NT // 2 - 1) as j:
                base = 8 * j
                norm(2 * j + 1, 1, j, base + 2)
                score(2 * j, 0, j, base + 4)
                norm(2 * j + 2, 0, j + 1, base + 6)
                score(2 * j + 1, 1, j, base + 8)
            j = NT // 2 - 1
            base = 8 * j
            norm(2 * j + 1, 1, j, base + 2)
            score(2 * j, 0, j, base + 4)
            score(2 * j + 1, 1, j, base + 6)

        @block.tensor
        def _(pe):
            pe.wait_ge(consts, 48)
            pe.wait_ge(ident_made, 2)
            with pe.Fori(0, NT // 2) as j:
                for b in range(2):
                    i = 2 * j + b
                    pe.wait_ge(xn_ready, i + 1)
                    pe.wait_ge(xT_copied, 2 * j)
                    for k in range(2):
                        last = nc.tensor.transpose(psT[:, b, k * NP:(k + 1) * NP], xn[0:NP, b, k * P:(k + 1) * P], ident[0:NP, 0:NP])
                    last.then_inc(xT_ready, 1)
                    pe.wait_ge(xT_copied, i + 1)
                    pe.wait_ge(hh_copied, 2 * j)
                    for k in range(2):
                        last = nc.tensor.matmul(psH[0:NP, b, 0:D], xnT[:, b, k, :], w[:, k, :], start=(k == 0), stop=(k == 1))
                    last.then_inc(hh_ready, 1)


QT, QE = TB // 4, P // 4
FRONT_LINKS, TILE_LINKS = 8, 2
SLOTS = 4
C1 = P + 1
TURN, SCORE, LAST, CARRY, REFER, WEIGH, SCALE = range(7)
STEPS = {0: [(TURN, 0)], 1: [(TURN, 1)], 2: [(TURN, 2)], 3: [(TURN, 3)], 7: [(SCORE, 0)], 9: [(LAST, 0)], 10: [(CARRY, 0)],
         12: [(REFER, 0)], 14: [(WEIGH, 0)], 15: [(SCALE, 0)]}


def wait(eng, s, value):
    if not isinstance(value, int) or value > 0:
        eng.wait_ge(s, value)


def pairs(eng, n, body):
    for b in range(2):
        body(0, b)
    with eng.Fori(1, n) as j:
        for b in range(2):
            body(j, b)


def load_values(nc, engine, at, n, greatest):
    _, values = nc.values_load_multi_w_load_instructions(
        at, engines=(engine,), min_val=0, max_val=greatest, skip_runtime_bounds_check_because="the inputs' kind bounds them")
    assert len(values) == n
    return values


def edge_stage(nc, table, sdst, srcT, dstT, dst_prev, firsts, lasts, acc):
    with ExitStack() as ctx:
        def sb(name, shape, dt=F32):
            return ctx.enter_context(nc.sbuf_tensor(name, shape, dt))

        def psum(name):
            return ctx.enter_context(nc.psum_tensor(name, [P, 512], F32))

        def sem(name):
            return ctx.enter_context(nc.semaphore(name))

        TH = TB * H
        assert TH == P and NB % 2 == 0 and TB % QT == 0  and TB % SLOTS == 0
        ident = sb("ident_e", [P, P])
        iota_i = sb("iota_i", [P, 5, P], I32)
        iota_f = sb("iota_f", [P, 5, P])
        head_i = sb("head_i", [P, 1], I32)
        head = sb("head", [P, 1])
        tmask = sb("tmask", [P, TB])
        hsel = sb("hsel", [P, H])
        hselT = sb("hselT", [H, P])
        hx = sb("hx", [P, 3, P])
        first_i = sb("first_i", [P, ET], I32)
        last_i = sb("last_i", [P, ET + 1], I32)
        rel = sb("rel", [P, ET])
        last_rel = sb("last_rel", [P, ET])
        same = sb("same", [P, ET])
        kc = sb("kc", [H, ET])
        idx = sb("idx", [P, 2, TB], I32)
        dprev = sb("dprev", [P, 2, P + 1], I32)
        other = sb("other", [P, 2, P], I32)
        sdw = sb("sdw", [P, 2, TB, H])
        G = sb("G", [P, 2, TB, ROW])
        S = sb("S", [P, 2, TB, C1])
        ST = sb("ST", [P, TB, P])
        kz = sb("kz", [P, P])
        z1 = sb("z1", [P, TH])
        z = sb("z", [P, TH])
        F = sb("F", [P, P])
        Lm = sb("Lm", [P, TB])
        Cb = sb("Cb", [H, 2, TB + 1])
        cm = sb("cm", [P, TB])
        carry = sb("carry", [P, 1])
        dz = sb("dz", [P, P + 1])
        ez = sb("ez", [P, P + 1])
        Xm = sb("Xm", [P, TB])
        Eb = sb("Eb", [P, 2, TH])
        XK = sb("XK", [P, 2, TB, 2, 3])
        tmp = sb("tmp", [P, 2, 3])
        V = sb("V", [P, 3])
        psA = [psum(f"psA{s}") for s in range(SLOTS)]
        psS = psum("psS")
        psD = psum("psD")
        psC = psum("psC")
        D_Z = slice(TH, 2 * TH)
        C_C, C_CT, C_E, C_X = slice(0, TB), slice(TB, 2 * TB), slice(2 * TB, 2 * TB + TH), slice(2 * TB + TH, 5 * TB + TH)

        ident_made = sem("ident_made_e")
        iota_made = sem("iota_made")
        tmask_made = sem("tmask_made")
        index_loaded = sem("index_loaded")
        idx_loaded = [sem(f"idx_loaded{b}") for b in range(2)]
        dst_loaded = [sem(f"dst_loaded{b}") for b in range(2)]
        sdw_loaded = [sem(f"sdw_loaded{b}") for b in range(2)]
        gathered = [sem(f"gathered{b}") for b in range(2)]
        dve_link = sem("dve_link_e")
        hsel_made = sem("hsel_made")
        hselT_ready = sem("hselT_ready")
        hselT_copied = sem("hselT_copied")
        other_made = [sem(f"other_made{b}") for b in range(2)]
        marks_made = [sem(f"marks_made{b}") for b in range(2)]
        S_made = sem("S_made")
        ST_ready = sem("ST_ready")
        ST_copied = sem("ST_copied")
        sd_ready = [sem(f"sd_ready{b}") for b in range(2)]
        z_ready = sem("z_ready")
        zT_ready = sem("zT_ready")
        L_ready = sem("L_ready")
        C_ready = sem("C_ready")
        Cb_ready = sem("Cb_ready")
        CT_ready = sem("CT_ready")
        dz_ready = sem("dz_ready")
        ez_ready = sem("ez_ready")
        Xm_ready = sem("Xm_ready")
        EX_ready = sem("EX_ready")
        EX_copied = sem("EX_copied")
        G_scaled = sem("G_scaled")
        G_used = [[sem(f"G_used{b}_{c}") for c in range(4)] for b in range(2)]
        acc_ready = sem("acc_ready")
        carried = sem("carried")
        acc_copied = sem("acc_copied")
        block = ctx.enter_context(nc.Block())

        def tiles(i):
            return bass.ds(i * TB, TB)

        def run(eng, front, tile, begin=lambda i: None):
            def both(i, b, q, last=False):
                begin(i)
                for t in range(TB):
                    for step, c in STEPS.get(t, []) if not last else []:
                        front(i + 1, 1 - b, q + b, step, c)
                    tile(i, b, t)

            for steps in STEPS.values():
                for step, c in steps:
                    front(0, 0, 0, step, c)
            both(0, 0, 0)
            both(1, 1, 0)
            with eng.Fori(1, NB // 2 - 1) as j:
                both(2 * j, 0, j)
                both(2 * j + 1, 1, j)
            both(NB - 2, 0, NB // 2 - 1)
            both(NB - 1, 1, NB // 2 - 1, last=True)

        @block.gpsimd
        def _(pool):
            make_identity(nc, pool, ident, ident_made)
            nc.gpsimd.iota(iota_i[:, 0, :], pattern=[[1, P]], base=0, channel_multiplier=0).then_inc(iota_made, 1)
            for k in range(2):
                nc.gpsimd.iota(iota_i[:, 1 + k, :], pattern=[[1, P // HD], [0, HD]], base=k * (P // HD),
                               channel_multiplier=0).then_inc(iota_made, 1)
            nc.gpsimd.iota(iota_i[:, 3, :], pattern=[[0, P // H], [1, H]], base=0, channel_multiplier=0).then_inc(iota_made, 1)
            nc.gpsimd.iota(iota_i[:, 4, :], pattern=[[0, P]], base=0, channel_multiplier=1).then_inc(iota_made, 1)
            nc.gpsimd.memset(tmask[:, :], 1.0).then_inc(tmask_made, 1)
            pool.wait_ge(tmask_made, 1)
            nc.gpsimd.affine_select(out=tmask[:, :], in_=tmask[:, :], compare_op=ALU.is_ge, fill=0.0, base=0,
                                    pattern=[[-H, TB]], channel_multiplier=1).then_inc(tmask_made, 1)
            pool.wait_ge(tmask_made, 2)
            nc.gpsimd.affine_select(out=tmask[:, :], in_=tmask[:, :], compare_op=ALU.is_ge, fill=0.0, base=H - 1,
                                    pattern=[[H, TB]], channel_multiplier=-1).then_inc(tmask_made, 1)

            def gathers(j, b):
                pool.wait_ge(idx_loaded[b], 16 * (j + 1))
                pool.wait_ge(dst_loaded[b], 16 * (j + 1))
                for t in range(TB):
                    if t % QT == 0:
                        wait(pool, G_used[b][t // QT], j)
                        e = t // QT * QE
                        nc.gpsimd.tensor_tensor(other[:, b, e:e + QE], dprev[:, b, e + 1:e + QE + 1], dprev[:, b, e:e + QE],
                                                ALU.subtract).then_inc(other_made[b], 1)
                    nc.gpsimd.indirect_dma_start(G[:, b, t, :], None, table,
                                                 bass.IndirectOffsetOnAxis(idx[:, b, t:t + 1], 0)).then_inc(gathered[b], 16)

            pairs(pool, NB // 2, gathers)

        @block.sync
        def _(sp):
            sp.dma_start(first_i[:, :], firsts[None, :].broadcast_to([P, ET])).then_inc(index_loaded, 16)
            sp.dma_start(last_i[:, :], lasts[None, :].broadcast_to([P, ET + 1])).then_inc(index_loaded, 16)
            sp.dma_start(rel[:, :].bitcast(I32), dstT).then_inc(index_loaded, 16)
            sp.wait_ge(index_loaded, 48)

            def loads(j, b):
                i = 2 * j + b
                at, row = (sp.snap(i * TB), sp.snap(i * TH)) if not isinstance(i, int) else (i * TB, i * TH)
                wait(sp, gathered[b], 16 * TB * j)
                sp.dma_start(idx[:, b, :], srcT[:, bass.ds(at, TB)]).then_inc(idx_loaded[b], 16)
                wait(sp, marks_made[b], j)
                sp.dma_start(dprev[:, b, :], dst_prev[bass.ds(row, TH), :]).then_inc(dst_loaded[b], 16)
                for c in range(0, TB, QT):
                    nodes = load_values(nc, mybir.EngineType.SP, first_i[0:1, bass.ds(at + c, QT)], QT, N)
                    if c == 0:
                        wait(sp, sd_ready[b], j)
                    for t in range(QT):
                        sp.dma_start(sdw[:, b, c + t, :], sdst[bass.ds(nodes[t], P), :]).then_inc(sdw_loaded[b], 16)

            pairs(sp, NB // 2, loads)

        @block.scalar
        def _(act):
            def front(i, b, q, step, c):
                if step == TURN:
                    act.wait_ge(ST_ready, 4 * i + c + 1)
                    if c == 0:
                        wait(act, sd_ready[1 - b], q + b)
                    nc.scalar.copy(ST[:, c * QT:(c + 1) * QT, :], psS[:, :].rearrange("p (t e) -> p t e", t=QT)).then_inc(ST_copied, 1)
                if step == WEIGH:
                    act.wait_ge(dz_ready, i + 1)
                    nc.scalar.activation(ez[:, :], dz[:, :], ACT.Exp).then_inc(ez_ready, 1)
                if step == SCALE:
                    act.wait_ge(EX_ready, i + 1)
                    wait(act, carried, TB * (i - 1))
                    nc.scalar.copy(Eb[:, b, :], psC[:, C_E])
                    nc.scalar.copy(XK[:, b, :, 0, :].rearrange("p t k -> p k t"),
                                   psC[:, C_X].rearrange("p (k t) -> p k t", k=3)).then_inc(EX_copied, 1)

            values = [None]

            def tile(i, b, t):
                if t % QT == 0:
                    values[0] = load_values(nc, mybir.EngineType.Activation, first_i[0:1, bass.ds(i * TB + t, QT)], QT, N)
                wait(act, acc_copied, TB * i + t)
                act.wait_ge(carried, TB * i + t + 1)
                nc.scalar.copy(acc[:, :, bass.ds(values[0][t % QT], P)],
                               psA[t % SLOTS][:, 0:3 * C1].rearrange("p (k n) -> p k n", k=3)[:, :, 0:P]).then_inc(acc_copied, 1)

            act.wait_ge(hselT_ready, 1)
            nc.scalar.copy(hselT[:, :], psC[0:H, 0:P]).then_inc(hselT_copied, 1)
            act.wait_ge(index_loaded, 48)
            run(act, front, tile)

        @block.vector
        def _(dve):
            setup = Link(dve, dve_link)
            dve.wait_ge(iota_made, 5)
            setup(nc.vector.tensor_copy(iota_f[:, :, :], iota_i[:, :, :]))
            setup.wait()
            setup(nc.vector.tensor_single_scalar(head_i[:, :], iota_i[:, 4, 0:1], H - 1, ALU.bitwise_and))
            setup.wait()
            setup(nc.vector.tensor_copy(head[:, :], head_i[:, :]))
            setup.wait()
            setup(nc.vector.tensor_scalar(hx[:, :, :], iota_f[:, 1:4, :], head[:, :], None, ALU.is_equal))
            nc.vector.tensor_scalar(hsel[:, :], iota_f[:, 0, 0:H], head[:, :], None, ALU.is_equal).then_inc(hsel_made, 1)
            dve.wait_ge(index_loaded, 48)
            setup(nc.vector.tensor_tensor(rel[:, :], rel[:, :].bitcast(I32), first_i[:, :], ALU.subtract))
            setup(nc.vector.tensor_tensor(last_rel[:, :], last_i[:, 1:ET + 1], first_i[:, :], ALU.subtract))
            setup(nc.vector.tensor_tensor(same[:, :], last_i[:, 1:ET + 1], last_i[:, 0:ET], ALU.is_equal))
            setup.wait()
            setup(nc.vector.tensor_scalar(kc[:, :], same[0:H, :], 1.0, BIG, ALU.subtract, ALU.mult))
            setup(nc.vector.memset(Cb[:, :, :], 0.0))
            setup(nc.vector.memset(V[:, :], 0.0))
            for s in range(SLOTS):
                setup(nc.vector.memset(psA[s][:, 2 * C1:3 * C1], 0.0))
            setup.wait()
            dve.wait_ge(tmask_made, 3)
            dve.wait_ge(hselT_copied, 1)

            SETUP = setup.n
            BATCH = FRONT_LINKS + TB * TILE_LINKS
            link = Link(dve, dve_link, SETUP)

            def begin(i):
                if isinstance(i, int) and i == 1:
                    assert link.base + link.n == SETUP + FRONT_LINKS + i * BATCH
                link.base, link.n = SETUP + FRONT_LINKS + i * BATCH, 0

            def front(i, b, q, step, c):
                if step == TURN and c == 0:
                    wait(dve, acc_ready, TB * (i - 1))
                    nc.vector.tensor_tensor(S[:, b, :, 0:P], iota_f[:, 0:1, :].broadcast_to([P, TB, P]),
                                            rel[:, tiles(i)][:, :, None].broadcast_to([P, TB, P]), ALU.is_equal)
                    nc.vector.tensor_tensor(S[:, b, :, P], rel[:, tiles(i)], last_rel[:, tiles(i)], ALU.is_equal).then_inc(S_made, 1)
                if step == SCORE:
                    dve.wait_ge(other_made[b], 4 * (q + 1))
                    nc.vector.tensor_scalar(kz[:, :], other[:, b, :], 0.0, -BIG, ALU.not_equal, ALU.mult).then_inc(marks_made[b], 1)
                    dve.wait_ge(gathered[b], 16 * TB * (q + 1))
                    dve.wait_ge(sd_ready[b], q + 1)
                    link(nc.vector.tensor_tensor(z1[:, :].rearrange("p (t h) -> p t h", t=TB), G[:, b, :, D:ROW],
                                                 psD[:, 0:TH].rearrange("p (t h) -> p t h", t=TB), ALU.add))
                    link.wait()
                    wait(dve, zT_ready, i)
                    nc.vector.scalar_tensor_tensor(out=z[:, :], in0=z1[:, :], scalar=0.2, in1=z1[:, :],
                                                   op0=ALU.mult, op1=ALU.max).then_inc(z_ready, 1)
                if step == LAST:
                    dve.wait_ge(zT_ready, i + 1)
                    dve.wait_ge(marks_made[b], q + 1)
                    link(nc.vector.tensor_tensor_scan(F[:, :], kz[:, :], psD[:, D_Z], -BIG, ALU.add, ALU.max))
                    link.wait()
                    nc.vector.tensor_scalar(Lm[:, :], tmask[:, :], F[:, P - 1:P], None, ALU.mult).then_inc(L_ready, 1)
                if step == CARRY:
                    dve.wait_ge(C_ready, i + 1)
                    link(nc.vector.tensor_copy(Cb[:, b, 0:1], Cb[:, 1 - b, TB:TB + 1]))
                    link.wait()
                    nc.vector.tensor_tensor_scan(Cb[:, b, 1:TB + 1], kc[:, tiles(i)], psC[0:H, C_C], Cb[:, b, 0:1],
                                                 ALU.add, ALU.max).then_inc(Cb_ready, 1)
                if step == REFER:
                    dve.wait_ge(CT_ready, i + 1)
                    link(nc.vector.tensor_tensor(cm[:, :], psC[:, C_CT], tmask[:, :], ALU.mult))
                    link.wait()
                    link(nc.vector.tensor_reduce(carry[:, :], cm[:, :], AX_X, ALU.add))
                    link.wait()
                    link(nc.vector.tensor_tensor_scan(F[:, :], kz[:, :], psD[:, D_Z], carry[:, :], ALU.add, ALU.max))
                    link.wait()
                    link(nc.vector.tensor_tensor_scan(F[:, P - 2::-1], kz[:, P - 1:0:-1], F[:, P - 2::-1], F[:, P - 1:P],
                                                      ALU.add, ALU.max))
                    link.wait()
                    nc.vector.scalar_tensor_tensor(out=dz[:, P:P + 1], in0=carry[:, :], scalar=kz[:, 0:1], in1=F[:, 0:1],
                                                   op0=ALU.add, op1=ALU.subtract)
                    nc.vector.tensor_tensor(dz[:, 0:P], psD[:, D_Z], F[:, :], ALU.subtract).then_inc(dz_ready, 1)
                if step == WEIGH:
                    dve.wait_ge(ez_ready, i + 1)
                    nc.vector.tensor_scalar(Xm[:, :], tmask[:, :], ez[:, P:P + 1], None, ALU.mult).then_inc(Xm_ready, 1)
                if step == SCALE:
                    dve.wait_ge(EX_copied, i + 1)
                    rows = G[:, b, :, 0:D].rearrange("p t (h d) -> p t h d", h=H)
                    link(nc.vector.tensor_tensor(XK[:, b, :, 1, :], XK[:, b, :, 0, :],
                                                 same[:, tiles(i)][:, :, None].broadcast_to([P, TB, 3]), ALU.mult))
                    nc.vector.tensor_tensor(rows, rows, Eb[:, b, :].rearrange("p (t h) -> p t h", t=TB)[:, :, :, None]
                                            .broadcast_to([P, TB, H, HD]), ALU.mult).then_inc(G_scaled, 1)

            def tile(i, b, t):
                sums = psA[t % SLOTS][:, 0:3 * C1].rearrange("p (k n) -> p k n", k=3)
                link.wait()
                wait(dve, carried, TB * i + t)
                link(nc.vector.tensor_tensor(tmp[:, :, :], V[:, None, :].broadcast_to([P, 2, 3]), XK[:, b, t, :, :], ALU.mult))
                dve.wait_ge(acc_ready, TB * i + t + 1)
                link.wait()
                link(nc.vector.tensor_tensor(sums[:, :, 0], sums[:, :, 0], tmp[:, 0, :], ALU.add))
                nc.vector.tensor_tensor(V[:, :], sums[:, :, P], tmp[:, 1, :], ALU.add).then_inc(carried, 1)

            run(dve, front, tile, begin)

        @block.tensor
        def _(pe):
            pe.wait_ge(ident_made, 2)
            pe.wait_ge(hsel_made, 1)
            nc.tensor.transpose(psC[0:H, 0:P], hsel[:, :], ident[:, :]).then_inc(hselT_ready, 1)
            pe.wait_ge(hselT_copied, 1)

            def front(i, b, q, step, c):
                if step == TURN:
                    pe.wait_ge(S_made, i + 1)
                    wait(pe, ST_copied, 4 * i + c)
                    for t in range(c * QT, (c + 1) * QT):
                        last = nc.tensor.transpose(psS[:, (t % QT) * P:(t % QT + 1) * P], S[:, b, t, 0:P], ident[:, :])
                    last.then_inc(ST_ready, 1)
                if step == SCORE:
                    pe.wait_ge(sdw_loaded[b], 16 * TB * (q + 1))
                    pe.wait_ge(ST_copied, 4 * (i + 1))
                    wait(pe, dz_ready, i)
                    for t in range(TB):
                        last = nc.tensor.matmul(psD[:, t * H:(t + 1) * H], ST[:, t, :], sdw[:, b, t, :], start=True, stop=True)
                    last.then_inc(sd_ready[b], 1)
                if step == LAST:
                    pe.wait_ge(z_ready, i + 1)
                    nc.tensor.transpose(psD[:, D_Z], z[:, :], ident[:, :]).then_inc(zT_ready, 1)
                if step == CARRY:
                    pe.wait_ge(L_ready, i + 1)
                    wait(pe, EX_copied, i)
                    nc.tensor.matmul(psC[0:H, C_C], hsel[:, :], Lm[:, :], start=True, stop=True).then_inc(C_ready, 1)
                if step == REFER:
                    pe.wait_ge(Cb_ready, i + 1)
                    nc.tensor.matmul(psC[:, C_CT], hselT[:, :], Cb[:, b, 0:TB], start=True, stop=True).then_inc(CT_ready, 1)
                if step == SCALE:
                    pe.wait_ge(Xm_ready, i + 1)
                    nc.tensor.transpose(psC[:, C_E], ez[:, 0:P], ident[:, :])
                    for k in range(3):
                        last = nc.tensor.matmul(psC[:, C_X.start + k * TB:C_X.start + (k + 1) * TB], hx[:, k, :], Xm[:, :],
                                                start=True, stop=True)
                    last.then_inc(EX_ready, 1)

            def tile(i, b, t):
                if t == 0:
                    pe.wait_ge(G_scaled, i + 1)
                wait(pe, acc_copied, TB * i + t - SLOTS + 1)
                for k in range(3):
                    lhs = G[:, b, t, k * P:(k + 1) * P] if k < 2 else Eb[:, b, t * H:(t + 1) * H]
                    out = psA[t % SLOTS][0:P if k < 2 else H, k * C1:(k + 1) * C1]
                    last = nc.tensor.matmul(out, lhs, S[:, b, t, :], start=True, stop=True)
                    if k == 1 and t % QT == QT - 1:
                        last.then_inc(G_used[b][t // QT], 1)
                last.then_inc(acc_ready, 1)

            run(pe, front, tile)


def settle_stage(nc, acc, xnorm, x, gamma, beta, Wg, bg, xall, logits, x2):
    with ExitStack() as ctx:
        def sb(name, shape, dt=F32):
            return ctx.enter_context(nc.sbuf_tensor(name, shape, dt))

        def psum(name):
            return ctx.enter_context(nc.psum_tensor(name, [P, 2, 512], F32))

        def sem(name):
            return ctx.enter_context(nc.semaphore(name))

        ident = sb("ident_s", [P, P])
        gb = sb("gb", [P, 2, D])
        wg = sb("wg", [P, KD, E])
        bgb = sb("bgb", [P, E])
        mhalf = sb("mhalf", [P, 1])
        stage = sb("stage", [P, 2, 3, NP])
        xn = sb("xn_s", [P, 2, D])
        xt = sb("xt_s", [P, 2, D])
        rl = sb("rl", [P, H])
        o = sb("o", [P, D])
        o2 = sb("o2", [P, D])
        t0 = sb("t0", [P, D])
        t1 = sb("t1", [P, D])
        t2 = sb("t2", [P, D])
        u = sb("u", [P, D])
        ex = sb("ex", [P, D])
        v = sb("v", [P, D])
        x2s = sb("x2s", [P, 2, D])
        xn2 = sb("xn2", [P, 2, D])
        xT = sb("xT_s", [P, 2, KD, NP])
        stat = sb("stat_s", [P, 6])
        mv = sb("mv_s", [P, 2, 2])
        ve = sb("ve", [P, 2])
        rstd = sb("rstd_s", [P, 2])
        waited = sb("waited_s", [P, 1])
        psF = psum("psF")
        psX = psum("psX")
        psL = psum("psL")

        ident_made = sem("ident_made_s")
        consts = sem("consts_s")
        mhalf_made = sem("mhalf_made")
        in_loaded = [sem(f"in_loaded{b}") for b in range(2)]
        stage_ready = sem("stage_ready")
        f_ready = sem("f_ready")
        f_used = sem("f_used")
        link_s = sem("link_s")
        ve_ready = sem("ve_ready")
        rstd_ready = sem("rstd_ready")
        u_ready = sem("u_ready")
        ex_ready = sem("ex_ready")
        x_used = [sem(f"x_used{b}") for b in range(2)]
        x2_stored = [sem(f"x2_stored{b}") for b in range(2)]
        xn2_ready = sem("xn2_ready")
        xn2_copied = sem("xn2_copied")
        xT_ready = sem("xT_ready_s")
        xT_copied = sem("xT_copied_s")
        l_ready = sem("l_ready")
        l_used = sem("l_used")
        block = ctx.enter_context(nc.Block())

        def wait(eng, s, value):
            if not isinstance(value, int) or value > 0:
                eng.wait_ge(s, value)

        def run(eng, main, late):
            main(0, 0, 0)
            with eng.Fori(0, NT // 2 - 1) as j:
                main(2 * j + 1, 1, j)
                late(2 * j, 0, j)
                main(2 * j + 2, 0, j + 1)
                late(2 * j + 1, 1, j)
            main(NT - 1, 1, NT // 2 - 1)
            late(NT - 2, 0, NT // 2 - 1)
            late(NT - 1, 1, NT // 2 - 1)

        @block.gpsimd
        def _(pool):
            make_identity(nc, pool, ident, ident_made)
            nc.gpsimd.memset(mhalf[:, :], -0.5).then_inc(mhalf_made, 1)
            pool.wait_ge(mhalf_made, 1)
            with pool.Fori(0, NT) as i:
                for n in range(2):
                    pool.wait_ge(ve_ready, 2 * i + n + 1)
                    nc.gpsimd.tensor_tensor(rstd[0:NP, n:n + 1], ve[0:NP, n:n + 1], mhalf[0:NP, :], ALU.pow).then_inc(rstd_ready, 1)

        @block.sync
        def _(sp):
            sp.dma_start(gb[:, 0, :], gamma[None, :].broadcast_to([P, D])).then_inc(consts, 16)
            sp.dma_start(gb[:, 1, :], beta[None, :].broadcast_to([P, D])).then_inc(consts, 16)
            sp.dma_start(bgb[:, :], bg[None, :].broadcast_to([P, E])).then_inc(consts, 16)
            sp.dma_start(wg[:, :, :], Wg.rearrange("(k p) e -> p k e", p=P)).then_inc(consts, 16)
            with sp.Fori(0, NT // 2) as j:
                for b in range(2):
                    first = sp.snap((2 * j + b) * NP)
                    sp.wait_ge(x_used[b], j)
                    sp.dma_start(xn[0:NP, b, :], xnorm[bass.ds(first, NP), :]).then_inc(in_loaded[b], 16)
                    sp.dma_start(xt[0:NP, b, :], x[bass.ds(first, NP), :]).then_inc(in_loaded[b], 16)

        @block.scalar
        def _(act):
            def fetch(i, b):
                first = act.snap(i * NP) if not isinstance(i, int) else i * NP
                wait(act, f_ready, i - 1)
                nc.scalar.copy(stage[:, b, :, :], acc[:, :, bass.ds(first, NP)]).then_inc(stage_ready, 1)

            def main(i, b, q):
                if not isinstance(i, int) or i + 1 < NT:
                    fetch(i + 1, 1 - b)
                act.wait_ge(u_ready, i + 1)
                nc.scalar.activation(ex[0:NP, :], u[0:NP, :], ACT.Exp).then_inc(ex_ready, 1)

            def late(i, b, q):
                first = act.snap(i * NP) if not isinstance(i, int) else i * NP
                act.wait_ge(xn2_ready, i + 1)
                act.dma_start(x2[bass.ds(first, NP), :], x2s[0:NP, b, :]).then_inc(x2_stored[b], 16)
                nc.scalar.copy(xall[0:NP, bass.ds(i, 1), :].rearrange("p a d -> p (a d)"), xn2[0:NP, b, :]).then_inc(xn2_copied, 1)
                act.wait_ge(xT_ready, i + 1)
                nc.scalar.copy(xT[:, b, :, :], psX[:, b, 0:KD * NP].rearrange("p (k n) -> p k n", k=KD)).then_inc(xT_copied, 1)

            fetch(0, 0)
            run(act, main, late)
            for b in range(2):
                act.wait_ge(x2_stored[b], 16 * (NT // 2))

        MAIN_LINKS = 11

        @block.vector
        def _(dve):
            dve.wait_ge(consts, 64)
            link = Link(dve, link_s)

            def norm(src, out, n, i, done=None):
                link(nc.vector.bn_stats(stat[0:NP, :], src))
                link.wait()
                nc.vector.memset(waited[:, :], 0.0)
                link(nc.vector.bn_aggr(mv[0:NP, n, :], stat[0:NP, :]))
                link.wait()
                nc.vector.tensor_scalar(ve[0:NP, n:n + 1], mv[0:NP, n, 1:2], EPS, None, ALU.add).then_inc(ve_ready, 1)
                dve.wait_ge(rstd_ready, 2 * i + n + 1)
                ins = nc.vector.tensor_scalar(out, src, mv[0:NP, n, 0:1], rstd[0:NP, n:n + 1], ALU.subtract, ALU.mult)
                if done is None:
                    link(ins)
                    link.wait()
                else:
                    ins.then_inc(done, 1)

            def main(i, b, q):
                link.base, link.n = i * MAIN_LINKS, 0
                dve.wait_ge(f_ready, i + 1)
                link(nc.vector.reciprocal(rl[0:NP, :], psF[0:NP, b, 2 * P:2 * P + H]))
                link.wait()
                nc.vector.tensor_tensor(o[0:NP, :].rearrange("p (h d) -> p h d", h=H),
                                        psF[0:NP, b, 0:D].rearrange("p (h d) -> p h d", h=H),
                                        rl[0:NP, :, None].broadcast_to([NP, H, HD]), ALU.mult).then_inc(f_used, 1)
                dve.wait_ge(f_used, i + 1)
                dve.wait_ge(in_loaded[b], 32 * (q + 1))
                link(nc.vector.tensor_tensor(o2[0:NP, :], o[0:NP, :], xn[0:NP, b, :], ALU.add))
                link.wait()
                norm(o2[0:NP, :], t0[0:NP, :], 0, i)
                link(nc.vector.tensor_tensor(t1[0:NP, :], t0[0:NP, :], gb[0:NP, 0, :], ALU.mult))
                link.wait()
                link(nc.vector.tensor_tensor(t2[0:NP, :], t1[0:NP, :], gb[0:NP, 1, :], ALU.add))
                link.wait()
                nc.vector.tensor_scalar(u[0:NP, :], t2[0:NP, :], 0.0, None, ALU.min).then_inc(u_ready, 1)
                link(nc.vector.scalar_tensor_tensor(out=v[0:NP, :], in0=t2[0:NP, :], scalar=0.0, in1=xt[0:NP, b, :],
                                                    op0=ALU.max, op1=ALU.add))
                link.wait()
                nc.vector.memset(waited[:, :], 0.0).then_inc(x_used[b], 1)
                dve.wait_ge(ex_ready, i + 1)
                wait(dve, x2_stored[b], 16 * q)
                link(nc.vector.scalar_tensor_tensor(out=x2s[0:NP, b, :], in0=ex[0:NP, :], scalar=-1.0, in1=v[0:NP, :],
                                                    op0=ALU.add, op1=ALU.add))
                link.wait()
                wait(dve, xn2_copied, i - 1)
                wait(dve, xT_ready, i - 1)
                norm(x2s[0:NP, b, :], xn2[0:NP, b, :], 1, i, xn2_ready)

            def late(i, b, q):
                dve.wait_ge(l_ready, i + 1)
                nc.vector.tensor_tensor(logits[0:NP, :, bass.ds(i, 1)].rearrange("p e a -> p (e a)"), psL[0:NP, b, 0:E],
                                        bgb[0:NP, :], ALU.add).then_inc(l_used, 1)

            run(dve, main, late)

        @block.tensor
        def _(pe):
            pe.wait_ge(ident_made, 2)
            pe.wait_ge(consts, 64)

            def main(i, b, q):
                pe.wait_ge(stage_ready, i + 1)
                wait(pe, f_used, i - 1)
                for k in range(3):
                    last = nc.tensor.transpose(psF[0:NP, b, k * P:(k + 1) * P], stage[:, b, k, :], ident[:, :])
                last.then_inc(f_ready, 1)

            def late(i, b, q):
                pe.wait_ge(xn2_ready, i + 1)
                wait(pe, xT_copied, i)
                for k in range(KD):
                    last = nc.tensor.transpose(psX[:, b, k * NP:(k + 1) * NP], xn2[0:NP, b, k * P:(k + 1) * P], ident[0:NP, 0:NP])
                last.then_inc(xT_ready, 1)
                pe.wait_ge(xT_copied, i + 1)
                wait(pe, l_used, i)
                for k in range(KD):
                    last = nc.tensor.matmul(psL[0:NP, b, 0:E], xT[:, b, k, :], wg[:, k, :], start=(k == 0), stop=(k == KD - 1))
                last.then_inc(l_ready, 1)

            run(pe, main, late)


def route_stage(nc, logits, xall, slot_rows, gates, pos, tile_expert, b2, b2b):
    with ExitStack() as ctx:
        def sb(name, shape, dt=F32):
            return ctx.enter_context(nc.sbuf_tensor(name, shape, dt))

        def sem(name):
            return ctx.enter_context(nc.semaphore(name))

        ET_ = [P, E, NT]
        rank_i = sb("rank_i", [P, E], I32)
        rank_f = sb("rank_f", [P, E])
        slot_i = sb("slot_i", [P, SLOT_TILES], I32)
        slot_f = sb("slot_f", [P, SLOT_TILES])
        tri = sb("tri", [P, P])
        ones = sb("ones", [P, P])
        top = sb("top", [P, 2, NT])
        hit = sb("hit", ET_)
        code = sb("code", ET_)
        best = sb("best", [P, NT])
        mark = sb("mark", [P, 2, E, NT])
        rest = sb("rest", ET_)
        both = sb("both", ET_)
        total = sb("total", ET_)
        keep = sb("keep", ET_)
        run_ = sb("run", ET_)
        place = sb("place", ET_)
        size_i = sb("size_i", [P, E], I32)
        size_j = sb("size_j", [P, E], I32)
        size = sb("size", [P, E])
        end = sb("end", [P, E])
        start = sb("start", [P, E])
        zero = sb("zero", [P, E])
        diff = sb("diff", [P, NT])
        e2 = sb("e2", [P, NT])
        den = sb("den", [P, NT])
        posf = sb("posf", [P, 2, NT])
        over = sb("over", [P, SLOT_TILES, E])
        count = sb("count", [P, SLOT_TILES])
        psR = ctx.enter_context(nc.psum_tensor("psR", [P, 512], F32))
        psT = ctx.enter_context(nc.psum_tensor("psTot", [P, 512], F32))

        made = sem("made")
        shifted = sem("shifted")
        tri_made = sem("tri_made")
        step = sem("step")
        diff_ready = sem("diff_ready")
        e2_ready = sem("e2_ready")
        both_ready = sem("both_ready")
        ranks_ready = sem("ranks_ready")
        pos_ready = sem("pos_ready")
        scattered = sem("scattered")
        loaded = sem("biases_loaded")
        block = ctx.enter_context(nc.Block())
        A = slice(0, NP)

        @block.sync
        def _(sp):
            sp.dma_start(b2b[:, :], b2.rearrange("e d -> (e d)")[None, :].broadcast_to([P, E * D])).then_inc(loaded, 16)
            sp.wait_ge(loaded, 16)

        @block.gpsimd
        def _(pool):
            nc.gpsimd.iota(rank_i[:, :], pattern=[[-1, E]], base=E, channel_multiplier=0).then_inc(made, 1)
            nc.gpsimd.iota(slot_i[:, :], pattern=[[P, SLOT_TILES]], base=0, channel_multiplier=0).then_inc(made, 1)
            nc.gpsimd.memset(ones[:, :], 1.0).then_inc(made, 1)
            nc.gpsimd.memset(tri[:, :], 1.0).then_inc(tri_made, 1)
            pool.wait_ge(tri_made, 1)
            nc.gpsimd.affine_select(out=tri[:, :], in_=tri[:, :], compare_op=ALU.is_gt, fill=0.0, base=0,
                                    pattern=[[1, P]], channel_multiplier=-1).then_inc(tri_made, 1)
            pool.wait_ge(pos_ready, 1)
            for t in range(NT):
                for k in range(2):
                    nc.gpsimd.indirect_dma_start(slot_rows, bass.IndirectOffsetOnAxis(pos[A, k, t:t + 1], 0), xall[A, t, :],
                                                 None).then_inc(scattered, 16)
            pool.wait_ge(scattered, 16 * 2 * NT)

        @block.scalar
        def _(act):
            act.wait_ge(diff_ready, 1)
            nc.scalar.activation(e2[A, :], diff[A, :], ACT.Exp).then_inc(e2_ready, 1)

        @block.tensor
        def _(pe):
            pe.wait_ge(tri_made, 2)
            pe.wait_ge(both_ready, 1)
            nc.tensor.matmul(psR[0:NP, 0:E * NT], tri[A, 0:NP], both[A, :, :].rearrange("p e t -> p (e t)"), start=True, stop=True)
            nc.tensor.matmul(psT[0:NP, 0:E * NT], ones[A, 0:NP], both[A, :, :].rearrange("p e t -> p (e t)"), start=True,
                             stop=True).then_inc(ranks_ready, 1)

        @block.vector
        def _(dve):
            link = Link(dve, step)

            def do(ins):
                link(ins)
                link.wait()

            V = nc.vector

            def by_t(a):
                return a.rearrange("p e t -> p t e")

            def over_e(a):
                return a[:, None, :].broadcast_to([NP, E, NT])

            dve.wait_ge(made, 3)
            do(V.tensor_copy(rank_f[:, :], rank_i[:, :]))
            do(V.tensor_copy(slot_f[:, :], slot_i[:, :]))
            src = logits
            for k in range(2):
                do(V.tensor_reduce(top[A, k, :], by_t(src[A, :, :]), AX_X, ALU.max))
                do(V.tensor_tensor(hit[A, :, :], src[A, :, :], over_e(top[A, k, :]), ALU.is_equal))
                do(V.tensor_tensor(code[A, :, :], hit[A, :, :], rank_f[A, :, None].broadcast_to([NP, E, NT]), ALU.mult))
                do(V.tensor_reduce(best[A, :], by_t(code[A, :, :]), AX_X, ALU.max))
                do(V.tensor_tensor(mark[A, k, :, :], over_e(best[A, :]), rank_f[A, :, None].broadcast_to([NP, E, NT]), ALU.is_equal))
                if k == 0:
                    do(V.scalar_tensor_tensor(out=rest[A, :, :], in0=mark[A, k, :, :], scalar=-BIG, in1=src[A, :, :],
                                              op0=ALU.mult, op1=ALU.add))
                    src = rest
            V.tensor_tensor(both[A, :, :], mark[A, 0, :, :], mark[A, 1, :, :], ALU.add).then_inc(both_ready, 1)
            V.tensor_tensor(diff[A, :], top[A, 1, :], top[A, 0, :], ALU.subtract).then_inc(diff_ready, 1)
            dve.wait_ge(e2_ready, 1)
            do(V.tensor_scalar(den[A, :], e2[A, :], 1.0, None, ALU.add))
            do(V.reciprocal(gates[A, 0, :], den[A, :]))
            do(V.tensor_tensor(gates[A, 1, :], e2[A, :], gates[A, 0, :], ALU.mult))
            dve.wait_ge(ranks_ready, 1)
            do(V.memset(keep[:, :, :], 1.0))
            do(V.memset(keep[:, :, 0:1], 0.0))
            do(V.memset(zero[:, :], 0.0))
            do(V.tensor_copy(total[A, :, :].rearrange("p e t -> p (e t)"), psT[A, 0:E * NT]))
            do(V.tensor_tensor_scan(run_[A, :, :].rearrange("p e t -> p (e t)"), keep[A, :, :].rearrange("p e t -> p (e t)"),
                                    total[A, :, :].rearrange("p e t -> p (e t)"), 0.0, ALU.mult, ALU.add))
            do(V.tensor_scalar(size_i[A, :], run_[A, :, NT - 1], float(P - 1), None, ALU.add))
            do(V.tensor_single_scalar(size_j[A, :], size_i[A, :], -P, ALU.bitwise_and))
            do(V.tensor_copy(size[A, :], size_j[A, :]))
            do(V.tensor_tensor_scan(end[A, :], size[A, :], zero[A, :], 0.0, ALU.add, ALU.add))
            do(V.tensor_tensor(start[A, :], end[A, :], size[A, :], ALU.subtract))
            do(V.tensor_tensor(place[A, :, :], run_[A, :, :], total[A, :, :], ALU.subtract))
            do(V.tensor_tensor(code[A, :, :].rearrange("p e t -> p (e t)"), place[A, :, :].rearrange("p e t -> p (e t)"),
                               psR[A, 0:E * NT], ALU.add))
            do(V.tensor_tensor(place[A, :, :], code[A, :, :], start[A, :, None].broadcast_to([NP, E, NT]), ALU.add))
            for k in range(2):
                do(V.tensor_tensor(code[A, :, :], place[A, :, :], mark[A, k, :, :], ALU.mult))
                do(V.tensor_reduce(posf[A, k, :], by_t(code[A, :, :]), AX_X, ALU.add))
            V.tensor_copy(pos[A, :, :], posf[A, :, :]).then_inc(pos_ready, 1)
            do(V.tensor_tensor(over[A, :, :], slot_f[A, :, None].broadcast_to([NP, SLOT_TILES, E]),
                               end[A, None, :].broadcast_to([NP, SLOT_TILES, E]), ALU.is_ge))
            do(V.tensor_reduce(count[A, :], over[A, :, :], AX_X, ALU.add))
            do(V.tensor_scalar(tile_expert[A, :], count[A, :], float(E - 1), None, ALU.min))


def expert_stage(nc, slot_rows, slot_out, tile_expert, W1, b1, W2, b2b):
    with ExitStack() as ctx:
        def sb(name, shape, dt=F32):
            return ctx.enter_context(nc.sbuf_tensor(name, shape, dt))

        def sem(name):
            return ctx.enter_context(nc.semaphore(name))

        ident = sb("ident_x", [P, P])
        w1 = sb("w1", [P, KD, E * FF])
        w2 = sb("w2", [P, KF, E * D])
        b1_rows = sb("b1_rows", [E * KF, P])
        b1T = sb("b1T", [P, E * KF])
        xs = sb("xs", [P, 2, D])
        xT = sb("xT_x", [P, 2, KD, P])
        hs = sb("hs", [P, FF])
        hT = sb("hT", [P, 2, KF, P])
        ys = sb("ys", [P, 2, D])
        psX = ctx.enter_context(nc.psum_tensor("psX_x", [P, 512], F32))
        psH = ctx.enter_context(nc.psum_tensor("psH_x", [P, FF // 512, 512], F32))
        psG = ctx.enter_context(nc.psum_tensor("psG", [P, FF // 512, 512], F32))
        psY = ctx.enter_context(nc.psum_tensor("psY", [P, 2, 512], F32))

        ident_made = sem("ident_made_x")
        weights = sem("weights")
        b1_loaded = sem("b1_loaded")
        b1_turned = sem("b1_turned")
        b1_copied = sem("b1_copied")
        x_loaded = [sem(f"xs_loaded{b}") for b in range(2)]
        x_used = [sem(f"xs_used{b}") for b in range(2)]
        xT_copied = sem("xT_copied_x")
        h_ready = sem("h_ready")
        h_copied = sem("h_copied")
        hT_ready = sem("hT_ready")
        gelu_done = sem("gelu_done")
        y_ready = sem("y_ready")
        y_done = sem("y_done")
        y_stored = [sem(f"y_stored{b}") for b in range(2)]
        block = ctx.enter_context(nc.Block())
        HALF = FF // 2
        MH = KF // 2

        def wait(eng, s, value):
            if not isinstance(value, int) or value > 0:
                eng.wait_ge(s, value)

        def run(eng, body):
            body(0, 0, 0, True, False)
            with eng.Fori(0, SLOT_TILES // 2 - 1) as j:
                body(2 * j + 1, 1, j, False, False)
                body(2 * j + 2, 0, j + 1, False, False)
            body(SLOT_TILES - 1, 1, SLOT_TILES // 2 - 1, False, True)

        def expert_of(eng, i):
            return eng.value_load(tile_expert[0:1, bass.ds(i, 1)], min_val=0, max_val=E - 1)

        @block.gpsimd
        def _(pool):
            make_identity(nc, pool, ident, ident_made)

        @block.sync
        def _(sp):
            sp.dma_start(b1_rows[:, :], b1.rearrange("e (m p) -> (e m) p", p=P)).then_inc(b1_loaded, 16)
            for k in range(KD):
                sp.dma_start(w1[:, k, :].rearrange("p (e n) -> p e n", e=E),
                             W1[:, k * P:(k + 1) * P, :].rearrange("e p n -> p e n")).then_inc(weights, 16)
            for m in range(KF):
                sp.dma_start(w2[:, m, :].rearrange("p (e n) -> p e n", e=E),
                             W2[:, m * P:(m + 1) * P, :].rearrange("e p n -> p e n")).then_inc(weights, 16)
            with sp.Fori(0, SLOT_TILES // 2) as j:
                for b in range(2):
                    first = sp.snap((2 * j + b) * P)
                    sp.wait_ge(x_used[b], j)
                    sp.dma_start(xs[:, b, :], slot_rows[bass.ds(first, P), :]).then_inc(x_loaded[b], 16)

        @block.scalar
        def _(act):
            def copy_x(i, b, q):
                act.wait_ge(x_used[b], q + 1)
                wait(act, h_ready, 2 * (i - 1))
                nc.scalar.copy(xT[:, b, :, :], psX[:, 0:KD * P].rearrange("p (k n) -> p k n", k=KD)).then_inc(xT_copied, 1)

            def body(i, b, q, first, last):
                if not last:
                    copy_x(i + 1, 1 - b, q + b)
                e = expert_of(act, i)
                wait(act, y_ready, i - 1)
                for n in range(2):
                    act.wait_ge(hT_ready, 2 * i + n + 1)
                    for m in range(n * MH, (n + 1) * MH):
                        done = nc.scalar.activation(hT[:, b, m, :], psG[:, n, (m - n * MH) * P:(m - n * MH + 1) * P], ACT.Gelu,
                                                    bias=b1T[:, bass.ds(e * KF + m, 1)])
                    done.then_inc(gelu_done, 1)
                if not first:
                    store(i - 1, 1 - b)

            def store(i, b):
                first_slot = i * P if isinstance(i, int) else act.snap(i * P)
                act.wait_ge(y_done, i + 1)
                act.dma_start(slot_out[bass.ds(first_slot, P), :], ys[:, b, :]).then_inc(y_stored[b], 16)

            act.wait_ge(b1_turned, 1)
            nc.scalar.copy(b1T[:, :], psY[:, 0, 0:E * KF]).then_inc(b1_copied, 1)
            act.wait_ge(b1_copied, 1)
            copy_x(0, 0, 0)
            run(act, body)
            store(SLOT_TILES - 1, 1)
            for b in range(2):
                act.wait_ge(y_stored[b], 16 * (SLOT_TILES // 2))

        @block.vector
        def _(dve):
            def finish(i, b, q):
                e = expert_of(dve, i)
                dve.wait_ge(y_ready, i + 1)
                wait(dve, y_stored[b], 16 * q)
                nc.vector.tensor_tensor(ys[:, b, :], psY[:, b, 0:D], b2b[:, bass.ds(e * D, D)], ALU.add).then_inc(y_done, 1)

            def body(i, b, q, first, last):
                for n in range(2):
                    dve.wait_ge(h_ready, 2 * i + n + 1)
                    wait(dve, hT_ready, 2 * i + n - 1 if not first else 0)
                    nc.vector.tensor_copy(hs[:, n * HALF:(n + 1) * HALF], psH[:, n, :]).then_inc(h_copied, 1)
                if not first:
                    finish(i - 1, 1 - b, q - 1 + b)

            run(dve, body)
            finish(SLOT_TILES - 1, 1, SLOT_TILES // 2 - 1)

        @block.tensor
        def _(pe):
            pe.wait_ge(ident_made, 2)

            def turn_x(i, b, q):
                pe.wait_ge(x_loaded[b], 16 * (q + 1))
                wait(pe, xT_copied, i)
                for k in range(KD):
                    done = nc.tensor.transpose(psX[:, k * P:(k + 1) * P], xs[:, b, k * P:(k + 1) * P], ident[:, :])
                done.then_inc(x_used[b], 1)

            def down(i, b, q):
                e = expert_of(pe, i)
                wait(pe, y_done, i)
                for m in range(KF):
                    if m % MH == 0:
                        pe.wait_ge(gelu_done, 2 * i + m // MH + 1)
                    done = nc.tensor.matmul(psY[:, b, 0:D], hT[:, b, m, :], w2[:, m, bass.ds(e * D, D)],
                                            start=(m == 0), stop=(m == KF - 1))
                done.then_inc(y_ready, 1)

            def body(i, b, q, first, last):
                e = expert_of(pe, i)
                pe.wait_ge(xT_copied, i + 1)
                for n in range(2):
                    wait(pe, h_copied, 2 * i + n - 1 if not first else 0)
                    for k in range(KD):
                        done = nc.tensor.matmul(psH[:, n, :], xT[:, b, k, :], w1[:, k, bass.ds(e * FF + n * HALF, HALF)],
                                                start=(k == 0), stop=(k == KD - 1))
                    done.then_inc(h_ready, 1)
                if not last:
                    turn_x(i + 1, 1 - b, q + b)
                if not first:
                    down(i - 1, 1 - b, q - 1 + b)
                for n in range(2):
                    pe.wait_ge(h_copied, 2 * i + n + 1)
                    wait(pe, gelu_done, 2 * i + n - 1 if not first else 0)
                    for m in range(n * MH, (n + 1) * MH):
                        done = nc.tensor.transpose(psG[:, n, (m - n * MH) * P:(m - n * MH + 1) * P], hs[:, m * P:(m + 1) * P],
                                                   ident[:, :])
                    done.then_inc(hT_ready, 1)

            pe.wait_ge(b1_loaded, 16)
            nc.tensor.transpose(psY[:, 0, 0:E * KF], b1_rows[:, :], ident[0:E * KF, 0:E * KF]).then_inc(b1_turned, 1)
            turn_x(0, 0, 0)
            pe.wait_ge(b1_copied, 1)
            pe.wait_ge(weights, 16 * (KD + KF))
            run(pe, body)
            down(SLOT_TILES - 1, 1, SLOT_TILES // 2 - 1)


def combine_stage(nc, slot_out, x2, gates, pos, out):
    RING = 4
    with ExitStack() as ctx:
        def sb(name, shape, dt=F32):
            return ctx.enter_context(nc.sbuf_tensor(name, shape, dt))

        def sem(name):
            return ctx.enter_context(nc.semaphore(name))

        y = sb("y_c", [P, RING, 2, D])
        xt = sb("xt_c", [P, RING, D])
        part = sb("part", [P, RING, D])
        res = sb("res", [P, RING, D])
        x_loaded = [sem(f"xc_loaded{r}") for r in range(RING)]
        y_loaded = [[sem(f"y{k}_loaded{r}") for r in range(RING)] for k in range(2)]
        half = sem("half")
        done = sem("done_c")
        stored = [sem(f"stored_c{r}") for r in range(RING)]
        block = ctx.enter_context(nc.Block())

        @block.gpsimd
        def _(pool):
            for t in range(NT):
                if t >= RING:
                    pool.wait_ge(done, t - RING + 1)
                for k in range(2):
                    nc.gpsimd.indirect_dma_start(y[0:NP, t % RING, k, :], None, slot_out,
                                                 bass.IndirectOffsetOnAxis(pos[0:NP, k, t:t + 1], 0)).then_inc(y_loaded[k][t % RING], 16)

        @block.sync
        def _(sp):
            for t in range(NT):
                if t >= RING:
                    sp.wait_ge(done, t - RING + 1)
                sp.dma_start(xt[0:NP, t % RING, :], x2[t * NP:(t + 1) * NP, :]).then_inc(x_loaded[t % RING], 16)

        @block.scalar
        def _(act):
            for t in range(NT):
                act.wait_ge(done, t + 1)
                act.dma_start(out[t * NP:(t + 1) * NP, :], res[0:NP, t % RING, :]).then_inc(stored[t % RING], 16)
            for r in range(RING):
                act.wait_ge(stored[r], 16 * len(range(r, NT, RING)))

        @block.vector
        def _(dve):
            for t in range(NT):
                r, n = t % RING, 16 * (t // RING + 1)
                dve.wait_ge(x_loaded[r], n)
                dve.wait_ge(y_loaded[0][r], n)
                nc.vector.scalar_tensor_tensor(out=part[0:NP, r, :], in0=y[0:NP, r, 0, :], scalar=gates[0:NP, 0, t:t + 1],
                                               in1=xt[0:NP, r, :], op0=ALU.mult, op1=ALU.add).then_inc(half, 1)
                dve.wait_ge(y_loaded[1][r], n)
                dve.wait_ge(half, t + 1)
                if t >= RING:
                    dve.wait_ge(stored[r], n - 16)
                nc.vector.scalar_tensor_tensor(out=res[0:NP, r, :], in0=y[0:NP, r, 1, :], scalar=gates[0:NP, 1, t:t + 1],
                                               in1=part[0:NP, r, :], op0=ALU.mult, op1=ALU.add).then_inc(done, 1)


def build(nc, x, srcT, dstT, dst_prev, firsts, lasts, W, a_src, a_dst, gamma, beta, Wg, bg, W1, b1, W2, b2, out):
    def dram(name, shape):
        return nc.dram_tensor(name, shape, F32, kind="Internal").ap()

    table = dram("table", (N, ROW))
    sdst = dram("sdst", (NPAD, H))
    xnorm = dram("xnorm", (N, D))
    x2 = dram("x2", (N, D))
    slot_rows = dram("slot_rows", (NSLOT, D))
    slot_out = dram("slot_out", (NSLOT, D))

    node_stage(nc, x, W, a_src, a_dst, table, sdst, xnorm, slot_rows)
    with ExitStack() as routing:
        def sb(name, shape, dt=F32):
            return routing.enter_context(nc.sbuf_tensor(name, shape, dt))

        gates = sb("gates", [P, 2, NT])
        pos = sb("pos", [P, 2, NT], I32)
        tile_expert = sb("tile_expert", [P, SLOT_TILES], I32)
        b2b = sb("b2b", [P, E * D])
        with ExitStack() as graph:
            acc = graph.enter_context(nc.sbuf_tensor("acc", [P, 3, NPAD], F32))
            edge_stage(nc, table, sdst, srcT, dstT, dst_prev, firsts, lasts, acc)
            xall = graph.enter_context(nc.sbuf_tensor("xall", [P, NT, D], F32))
            logits = graph.enter_context(nc.sbuf_tensor("logits", [P, E, NT], F32))
            settle_stage(nc, acc, xnorm, x, gamma, beta, Wg, bg, xall, logits, x2)
            route_stage(nc, logits, xall, slot_rows, gates, pos, tile_expert, b2, b2b)
        expert_stage(nc, slot_rows, slot_out, tile_expert, W1, b1, W2, b2b)
        combine_stage(nc, slot_out, x2, gates, pos, out)


def kernel(**inputs):
    import numpy as np
    import concourse.bacc as bacc
    from concourse.bass_utils import run_bass_kernel_spmd

    fill = ET * P - EDGES
    src = np.concatenate([np.asarray(inputs["src"]), np.zeros(fill, np.int32)])
    dst = np.concatenate([np.asarray(inputs["dst"]), np.full(fill, N, np.int32)])
    by_tile = dst.reshape(ET, P)
    lasts = np.concatenate([np.full(1, -1, np.int32), by_tile[:, P - 1]])
    prev = np.concatenate([lasts[:ET, None], by_tile], axis=1)
    arrays = {
        "in_x": inputs["x"],
        "in_srcT": src.reshape(ET, P).T,
        "in_dstT": by_tile.T,
        "in_dst_prev": np.repeat(prev, H, axis=0),
        "in_firsts": by_tile[:, 0],
        "in_lasts": lasts,
    }
    for name in ("gnn_W", "gnn_a_src", "gnn_a_dst", "gnn_gamma", "gnn_beta", "ffn_Wg", "ffn_bg", "ffn_W1", "ffn_b1", "ffn_W2", "ffn_b2"):
        arrays["in_" + name] = inputs["L0_" + name]
    arrays = {k: np.ascontiguousarray(v) for k, v in arrays.items()}

    nc = bacc.Bacc("TRN2", target_bir_lowering=False, num_devices=1)
    args = [nc.dram_tensor(k, a.shape, mybir.dt.from_np(a.dtype), kind="ExternalInput").ap() for k, a in arrays.items()]
    out = nc.dram_tensor("out", (N, D), F32, kind="ExternalOutput").ap()
    build(nc, *args, out)
    r = run_bass_kernel_spmd(nc, [arrays], core_ids=[0])
    return r.results[0]["out"]
```
